# Optimizing a Trainium2 kernel written in Bass

```python
import numpy as np
import jax
import jax.numpy as jnp

def _softmax(x, axis=-1):
    return jax.nn.softmax(x, axis=axis)

def _gelu(x):
    return jax.nn.gelu(x, approximate=True)

def _silu(x):
    return jax.nn.silu(x)

def _sigmoid(x):
    return jax.nn.sigmoid(x)

def _layernorm(x, axis=-1, eps=1e-05):
    m = jnp.mean(x, axis=axis, keepdims=True)
    v = jnp.var(x, axis=axis, keepdims=True)
    return (x - m) / jnp.sqrt(v + eps)

def _scatter_add(tgt, idx, src, axis=0):
    return tgt.at[idx].add(src)

def _segment_sum(src, seg, n):
    return jax.ops.segment_sum(src, seg, n)
kernel_name = 'mk_gnn_preln_d2_gnn_r8_67fe4c'

def setup_inputs(seed: int=0):
    np.random.seed(seed)
    _w = jnp.asarray

    def _rec_inputs():
        import jax
        import jax.numpy as jnp
        _gk = jax.random.key(seed)
        x = -0.0002928 + 1 * jax.random.normal(jax.random.fold_in(_gk, 1), (1024, 512), jnp.float32)
        _s = jax.random.randint(jax.random.fold_in(_gk, 2), (16384,), 0, 1024, jnp.int32)
        _d = jax.random.randint(jax.random.fold_in(_gk, 3), (16384,), 0, 1024, jnp.int32)
        _loop = jnp.arange(1024, dtype=jnp.int32)
        src = jnp.concatenate([_s, _d, _loop])
        dst = jnp.concatenate([_d, _s, _loop])
        _o = jnp.argsort(dst, stable=True)
        src = src[_o]
        dst = dst[_o]
        return (x, src, dst)
    x, src, dst = _rec_inputs()

    def _L0_gnn_setup():
        import jax, jax.numpy as jnp
        import numpy as np
        NEG = -1000000.0
        key = jax.random.key(seed)
        ks = jax.random.split(key, 8)
        N, D_IN, D_Q, D_K, E = (1024, 512, 512, 512, 32768)
        s = 1.0 / np.sqrt(D_IN)
        return {'x': jax.random.normal(ks[0], (N, D_IN), dtype=jnp.float32), 'edge_index': jax.random.randint(ks[1], (2, E), 0, N, dtype=jnp.int64), 'Wq': jax.random.normal(ks[2], (D_IN, D_Q), dtype=jnp.float32) * s, 'bq': jax.random.normal(ks[3], (D_Q,), dtype=jnp.float32) * 0.01, 'Wk': jax.random.normal(ks[4], (D_IN, D_K), dtype=jnp.float32) * s, 'bk': jax.random.normal(ks[5], (D_K,), dtype=jnp.float32) * 0.01, 'Wv': jax.random.normal(ks[6], (D_IN, D_K), dtype=jnp.float32) * s, 'bv': jax.random.normal(ks[7], (D_K,), dtype=jnp.float32) * 0.01}
    _L0_gnn_all = _L0_gnn_setup()
    _L0_gnn_in = {k: v for k, v in _L0_gnn_all.items() if k in ('Wq', 'bq', 'Wk', 'bk', 'Wv', 'bv')}
    del _L0_gnn_all

    def _L1_gnn_setup():
        import jax, jax.numpy as jnp
        import numpy as np
        N = 6250
        DIM = 512
        E = 18750
        key = jax.random.key(seed)
        k_x, k_src, k_dst, k_w, k_b = jax.random.split(key, 5)
        x = jax.random.normal(k_x, (N, DIM), dtype=jnp.float32)
        src = jax.random.randint(k_src, (E,), 0, N)
        dst = jax.random.randint(k_dst, (E,), 0, N)
        edge_index = jnp.stack([src, dst], axis=0)
        bound = 1.0 / np.sqrt(DIM)
        W = jax.random.uniform(k_w, (DIM, DIM), minval=-bound, maxval=bound, dtype=jnp.float32)
        b = jax.random.uniform(k_b, (DIM,), minval=-bound, maxval=bound, dtype=jnp.float32)
        alpha = jnp.float32(0.5)
        return {'x': x, 'edge_index': edge_index, 'num_nodes': N, 'alpha': alpha, 'W': W, 'b': b}
    _L1_gnn_all = _L1_gnn_setup()
    _L1_gnn_in = {k: v for k, v in _L1_gnn_all.items() if k in ('alpha', 'W', 'b')}
    del _L1_gnn_all
    return {'x': x, 'src': src, 'dst': dst, 'L0_gnn_Wq': _L0_gnn_in['Wq'], 'L0_gnn_bq': _L0_gnn_in['bq'], 'L0_gnn_Wk': _L0_gnn_in['Wk'], 'L0_gnn_bk': _L0_gnn_in['bk'], 'L0_gnn_Wv': _L0_gnn_in['Wv'], 'L0_gnn_bv': _L0_gnn_in['bv'], 'L1_gnn_alpha': _L1_gnn_in['alpha'], 'L1_gnn_W': _L1_gnn_in['W'], 'L1_gnn_b': _L1_gnn_in['b']}

def reference(x, src, dst, L0_gnn_Wq, L0_gnn_bq, L0_gnn_Wk, L0_gnn_bk, L0_gnn_Wv, L0_gnn_bv, L1_gnn_alpha, L1_gnn_W, L1_gnn_b):
    import jax
    import jax.numpy as jnp

    def _L0_gnn_ref(x, edge_index, Wq, bq, Wk, bk, Wv, bv):
        import jax, jax.numpy as jnp
        import numpy as np
        NEG = -1000000.0
        q = x @ Wq + bq
        k = x @ Wk + bk
        v = x @ Wv + bv
        N = x.shape[0]
        adj = jnp.zeros((N, N), dtype=x.dtype).at[edge_index[0], edge_index[1]].set(1.0)
        a = q @ k.T / jnp.sqrt(jnp.asarray(q.shape[-1], dtype=x.dtype))
        a = a * adj + (1.0 - adj) * NEG
        attn = jax.nn.softmax(a, axis=-1)
        return attn @ v

    def _L1_gnn_ref(x, edge_index, num_nodes, alpha, W, b):
        import jax, jax.numpy as jnp
        import numpy as np
        N = 6250
        DIM = 512
        E = 18750
        src = edge_index[0]
        dst = edge_index[1]
        agg = jax.ops.segment_sum(x[src], dst, num_segments=num_nodes)
        deg = jax.ops.segment_sum(jnp.ones_like(dst, dtype=x.dtype), dst, num_segments=num_nodes)
        deg = jnp.maximum(deg, 1.0)
        agg = agg / deg[:, None]
        return x + alpha * (agg @ W.T + b)
    edge_index = jnp.stack([src, dst])
    h = jnp.maximum(_layernorm(x, axis=-1), 0.0)
    x = x + _L0_gnn_ref(h, edge_index, L0_gnn_Wq, L0_gnn_bq, L0_gnn_Wk, L0_gnn_bk, L0_gnn_Wv, L0_gnn_bv)
    h = jnp.maximum(_layernorm(x, axis=-1), 0.0)
    x = x + _L1_gnn_ref(h, edge_index, 1024, L1_gnn_alpha, L1_gnn_W, L1_gnn_b)
    return x

_drawn_inputs = setup_inputs


def setup_inputs(seed=0):
    import zlib

    import numpy as np

    out = dict(_drawn_inputs(seed))
    spreads = {}
    factors = {'L0_gnn_bq': 64.0, 'L0_gnn_bk': 64.0, 'L0_gnn_bv': 6.21, 'L1_gnn_b': 7.539}
    for name, (base, spread) in spreads.items():
        noise = np.random.default_rng([zlib.crc32(name.encode()), seed]).standard_normal(out[name].shape)
        drawn = base * np.exp(spread * noise) if base else spread * noise
        out[name] = jnp.asarray(drawn.astype(out[name].dtype))
    for name, factor in factors.items():
        out[name] = (out[name] * factor).astype(out[name].dtype)
    return out
```

```python
import concourse.bass as bass
from concourse import mybir
from contextlib import ExitStack

F32 = mybir.dt.float32
F32R = mybir.dt.float32r
BF16 = mybir.dt.bfloat16
I32 = mybir.dt.int32
I8 = mybir.dt.int8
ALU = mybir.AluOpType
ACT = mybir.ActivationFunctionType
AX = mybir.AxisListType

P = 128
N, D, E = 1024, 512, 33792
NT = N // P
KD = D // P
ET = E // P
HALF = N // 2
NEG = -1.0e6
EPS = 1e-5
SCALE = 1.0 / float(D) ** 0.5

WIN = 32
GRP = 64
NG = N // GRP
TPB = 33
WSTEP, WBACK = 4, 16
EXACT = 4096

PAIRS = ET // 2
RING = 7


def window(t):
    return min(max(P * (t // TPB) + WSTEP * (t % TPB) - WBACK, 0), N - WIN)


def pieces(t):
    w = window(t)
    return [(g, max(w, GRP * g), min(w + WIN, GRP * g + GRP)) for g in range(w // GRP, (w + WIN - 1) // GRP + 1)]


FIRST = {g: min(t for t in range(ET) if any(p[0] == g for p in pieces(t))) for g in range(NG)}
LAST = {g: max(t for t in range(ET) if any(p[0] == g for p in pieces(t))) for g in range(NG)}


def schedule():
    dense = [("M", m) for m in range(KD)] + [("vec", 0), ("wv", 0)]
    dense += [("T", t) for t in range(4)] + [("G", m) for m in range(KD)]
    dense += [("T", t) for t in range(4, 8)] + [("G", KD + m) for m in range(KD)]
    dense += [("c", 0)] + [("V", t) for t in range(NT)]
    cost = {"M": 5, "G": 5, "V": 6, "T": 2, "vec": 4, "wv": 0, "c": 4}
    steps, at = [("splitw", 0)], 0
    steps += [("ln", 0), ("ln", 1)]
    lns = list(range(2, NT))

    def count(n):
        nonlocal at
        if at < PAIRS and n:
            steps.append(("count", at, min(at + n, PAIRS)))
            at = min(at + n, PAIRS)

    count(6)
    for s in dense:
        if lns and s[0] in ("M", "T", "vec"):
            steps.append(("ln", lns.pop(0)))
        steps.append(s)
        count(cost[s[0]])
    while at < PAIRS:
        count(6)
    return steps


STEPS = schedule()
VSTEPS = list(STEPS)
for _i in range(1, len(VSTEPS)):
    if VSTEPS[_i][0] == "count" and VSTEPS[_i - 1][0] not in ("count", "splitw"):
        VSTEPS[_i - 1], VSTEPS[_i] = VSTEPS[_i], VSTEPS[_i - 1]
PROJ = [s for s in STEPS if s[0] in ("M", "vec", "G", "c", "V")]
NPROJ = len(PROJ)


def hi_before(n):
    return sum(s[0] in ("M", "G", "V") for s in PROJ[:n])


def gnn_kernel(nc, x_d, src_d, dst_d, wqT_d, wkT_d, wv_d, wT_d, bq_d, bk_d, bv_d, b_d, alpha_d, out_d):
    with ExitStack() as ctx:
        base = ctx.enter_context(nc.sbuf_tensor("arena", [P, 53150], F32))
        top = nc.sbuf_base
        start = top - 53150 * 4
        at = [start + (-start) % 32]

        def region(nbytes):
            a = at[0]
            at[0] += (nbytes + 31) // 32 * 32
            assert at[0] <= top, (at[0], top)
            return a

        def place(name, shape, dt, offset):
            return nc.alloc_sbuf_tensor_at(name, shape, dt, offset=offset)

        def small(name, shape, dt):
            size = 2 if dt == BF16 else 4
            for s in shape[1:]:
                size *= s
            return place(name, shape, dt, region(size))

        KB = 1024
        r_hT, r_G, r_V, r_A = (region(32 * KB) for _ in range(4))
        r_x, r_W0, r_W2, r_W1, r_R = region(16 * KB), region(16 * KB), region(16 * KB), region(16 * KB), region(8 * KB)

        hT = [place("hT_hi", [P, KD, N], F32R, r_hT), place("hT_lo", [P, KD, N], F32R, r_hT + 16 * KB)]
        agT = [place("agT_hi", [P, KD, N], F32R, r_hT), place("agT_lo", [P, KD, N], F32R, r_hT + 16 * KB)]
        GT = [place("GT_hi", [P, NT, KD, P], F32R, r_G), place("GT_lo", [P, NT, KD, P], F32R, r_G + 16 * KB)]
        h2 = [place("h2_hi", [P, NT, D], F32R, r_G), place("h2_lo", [P, NT, D], F32R, r_G + 16 * KB)]
        iota_i = place("iota_i", [P, 512], I32, r_G)
        win0 = place("win0", [P, ET], F32, r_G + 2 * KB)
        key_t = [place(f"key_t{i}", [P, ET], F32, r_G + (4 + 2 * i) * KB) for i in range(4)]
        key_i = [place(f"key_i{i}", [P, ET], I32, r_G + (12 + 2 * i) * KB) for i in range(2)]
        V = [place("V_hi", [P, NT, D], F32R, r_V), place("V_lo", [P, NT, D], F32R, r_V + 16 * KB)]
        h1 = place("h1", [P, NT, D], F32, r_V)
        wk = [place("wk_hi", [P, KD, D], F32R, r_V + 16 * KB), place("wk_lo", [P, KD, D], F32R, r_V + 24 * KB)]
        wk_raw = place("wk_raw", [P, KD, D], F32, r_V + 24 * KB)
        o_sb = place("o_sb", [P, NT, D], F32, r_V)
        A = place("A", [P, NT, N], F32R, r_A)
        A_f = A[:, :, :].bitcast(F32)
        A_i = A[:, :, :].bitcast(I32)
        R = place("R", [P, NT, N], I8, r_R)
        xs = place("xs", [P, NT, D], F32, r_x)
        wq = [place("wq_hi", [P, KD, D], F32R, r_W0), place("wq_lo", [P, KD, D], F32R, r_W0 + 8 * KB)]
        wq_raw = place("wq_raw", [P, KD, D], F32, r_W0 + 8 * KB)
        wv = [place("wv_hi", [P, KD, D], F32R, r_W0), place("wv_lo", [P, KD, D], F32R, r_W0 + 8 * KB)]
        wv_raw = place("wv_raw", [P, KD, D], F32, r_W0 + 8 * KB)
        M = [place("M_hi", [P, KD, D], F32R, r_W2), place("M_lo", [P, KD, D], F32R, r_W2 + 8 * KB)]
        pr = [place(f"pr{i}", [P, N], F32, r_W0 + 4 * KB * i) for i in range(2)]
        pT = [[place(f"pT_hi{i}", [P, NT, P], F32R, r_W0 + (8 + 8 * i) * KB),
               place(f"pT_lo{i}", [P, NT, P], F32R, r_W0 + (12 + 8 * i) * KB)] for i in range(2)]
        h2f = [place(f"h2f{i}", [P, D], F32, r_W0 + (24 + 2 * i) * KB) for i in range(2)]
        r_st = [place(f"r_st{i}", [P, HALF], F32R, r_W0 + (24 + 2 * i) * KB) for i in range(2)]
        b_sb = place("b_sb", [P, D], F32, r_W0 + 28 * KB)
        ohL = place("ohL", [P, RING, 2, P], BF16, r_W1)
        ohW = place("ohW", [P, RING, 2, NT, WIN], BF16, r_W1 + RING * 2 * P * 2)
        bv_sb = place("bv_sb", [P, D], F32, r_W1 + 11 * KB)
        iotaG = place("iotaG", [P, NT, GRP], F32, r_W1 + 13 * KB)
        genL = place("genL", [P, 2, P], BF16, r_W1)
        genW = place("genW", [P, 2, NT * GRP], BF16, r_W1 + 1 * KB)
        gen0 = place("gen0", [P, NT * GRP], BF16, r_W1 + 3 * KB)
        gen_key = place("gen_key", [P, ET], F32, r_W1 + 4 * KB)
        gen_i = place("gen_i", [P, ET], I32, r_W1 + 6 * KB)
        gen_R = place("gen_R", [P, N], F32R, r_W1 + 6 * KB)
        wt = [place("wt_hi", [P, KD, D], F32R, r_W1), place("wt_lo", [P, KD, D], F32R, r_W1 + 8 * KB)]
        wt_raw = place("wt_raw", [P, KD, D], F32, r_W1 + 8 * KB)

        src_i, dst_i = small("src_i", [P, ET], I32), small("dst_i", [P, ET], I32)
        lo_f, key_f = small("lo_f", [P, ET], F32), small("key_f", [P, ET], F32)
        iotaL, iotaW = small("iotaL", [P, P], BF16), small("iotaW", [P, NT * WIN], BF16)
        ident, ones_f = small("ident", [P, P], F32), small("ones_f", [P, P], F32)
        ones_r = small("ones_r", [P, 2], F32R)
        bqk = small("bqk", [P, 2, KD], F32)
        bqk_r = small("bqk_r", [P, 2, KD, 2], F32R)
        bqk_z = small("bqk_z", [P, 2, KD, 2], F32R)
        bprod = small("bprod", [P, KD], F32)
        u_f, g0 = small("u_f", [P, KD], F32), small("g0", [P, KD], F32)
        u_r, u_z = small("u_r", [P, KD, 2], F32R), small("u_z", [P, KD, 2], F32R)
        bb, c_f, negc = small("bb", [P, 1], F32), small("c_f", [P, NT], F32), small("negc", [P, NT], F32)
        bn = small("bn", [P, 2, NT, 6], F32)
        mv = small("mv", [P, 2, NT, 2], F32)
        nhalf = small("nhalf", [P, 1], F32)
        var_e, rstd, nmr = (small(n, [P, 2, NT], F32) for n in ("var_e", "rstd", "nmr"))
        negmax, rowsum, rinv = (small(n, [P, NT], F32) for n in ("negmax", "rowsum", "rinv"))
        deg, rdeg = small("deg", [P, NT], F32), small("rdeg", [P, NT], F32)
        alpha = small("alpha", [P, 1], F32)
        stat, found = small("stat", [P, 2], F32), small("found", [P, 2], F32)
        dmax = small("dmax", [P, 1], F32)
        flag = small("flag", [P, 1], I32)

        bank = [ctx.enter_context(nc.psum_tensor(f"bank{i}", [P, 512], F32)) for i in range(8)]

        def sem(name):
            return ctx.enter_context(nc.semaphore(name))

        ld_edges, ld_wq, ld_wk, ld_wv, ld_wt = (sem(n) for n in ("ld_edges", "ld_wq", "ld_wk", "ld_wv", "ld_wt"))
        ld_x = [sem(f"ld_x{i}") for i in range(4)]
        ld_bqk, ld_bv, ld_b, stored = sem("ld_bqk"), sem("ld_bv"), sem("ld_b"), sem("stored")
        consts = sem("consts")
        pool_chain, dve_chain = sem("pool_chain"), sem("dve_chain")
        oh_ready, oh_used = sem("oh_ready"), sem("oh_used")
        count_kept = sem("count_kept")
        w_hi, w_lo = sem("w_hi"), sem("w_lo")
        vec_ready = sem("vec_ready")
        stats, normed, relu = sem("stats"), sem("normed"), sem("relu")
        hT_ps, hT_hi, hT_lo = sem("hT_ps"), sem("hT_hi"), sem("hT_lo")
        proj, proj_hi, proj_lo = sem("proj"), sem("proj_hi"), sem("proj_lo")
        res_ready = sem("res_ready")
        deg_ps, stat_ready, stat_ps, flag_ready = sem("deg_ps"), sem("stat_ready"), sem("stat_ps"), sem("flag_ready")
        counts_final = sem("counts_final")
        gen_ready, gen_used, gen_ps, gen_A, gen_R_s = (sem(n) for n in ("gen_ready", "gen_used", "gen_ps", "gen_A", "gen_R_s"))
        gen_prep, gen_iota, gen_stage, gen_deg = (sem(n) for n in ("gen_prep", "gen_iota", "gen_stage", "gen_deg"))
        agg_stage, agg_used = sem("agg_stage"), sem("agg_used")
        filled, scored, masked, maxed, expd = (sem(n) for n in ("filled", "scored", "masked", "maxed", "expd"))
        pT_ps, pT_hi, pT_lo = sem("pT_ps"), sem("pT_hi"), sem("pT_lo")
        attended, x2_ready, h2_hi, h2_lo, res2_ready = (sem(n) for n in ("attended", "x2_ready", "h2_hi", "h2_lo", "res2_ready"))
        agg_ps, agg_hi, agg_lo = sem("agg_ps"), sem("agg_hi"), sem("agg_lo")
        rdeg_ready, out_ps, out_ready = sem("rdeg_ready"), sem("out_ps"), sem("out_ready")

        def part(T, hl, *ix):
            return T[hl].__getitem__(ix)

        def f(ap):
            return ap.bitcast(F32)

        def proj_index(step):
            return PROJ.index(step)

        block = ctx.enter_context(nc.Block())

        @block.sync
        def _(sp):
            sp.dma_start(dst_i[:, :], dst_d).then_inc(ld_edges, 16)
            sp.dma_start(src_i[:, :], src_d).then_inc(ld_edges, 16)
            sp.dma_start(wq_raw[:, :, :], wqT_d.rearrange("(k p) n -> p k n", p=P)).then_inc(ld_wq, 16)
            sp.dma_start(wk_raw[:, :, :], wkT_d.rearrange("(k p) n -> p k n", p=P)).then_inc(ld_wk, 16)
            for i in range(4):
                sp.dma_start(xs[:, 2 * i:2 * i + 2, :],
                             x_d[2 * i * P:(2 * i + 2) * P, :].rearrange("(t p) n -> p t n", p=P)).then_inc(ld_x[i], 16)
            sp.dma_start(bv_sb[:, :], bv_d.partition_broadcast(P)).then_inc(ld_bv, 16)
            sp.wait_ge(proj, proj_index(("vec", 0)) + 1)
            sp.dma_start(wv_raw[:, :, :], wv_d.rearrange("(k p) n -> p k n", p=P)).then_inc(ld_wv, 16)
            sp.wait_ge(proj, NPROJ)
            sp.dma_start(b_sb[:, :], b_d.partition_broadcast(P)).then_inc(ld_b, 16)
            sp.wait_ge(counts_final, 1)
            sp.wait_ge(res_ready, NT)
            sp.dma_start(wt_raw[:, :, :], wT_d.rearrange("(k p) n -> p k n", p=P)).then_inc(ld_wt, 16)
            for j in range(NT):
                sp.wait_ge(out_ready, j + 1)
                sp.dma_start(out_d[j * P:(j + 1) * P, :], o_sb[:, j, :]).then_inc(stored, 16)
            sp.wait_ge(stored, 16 * NT)

        @block.gpsimd
        def _(pool):
            chain = [0]

            def link(ins):
                chain[0] += 1
                ins.then_inc(pool_chain, 1)
                pool.wait_ge(pool_chain, chain[0])

            link(nc.gpsimd.iota(iota_i[:, 0:ET], [[P, ET // TPB], [WSTEP, TPB]], base=-WBACK, channel_multiplier=0))
            nc.gpsimd.tensor_scalar(win0[:, :], iota_i[:, 0:ET], 0.0, float(N - WIN), ALU.max, ALU.min).then_inc(consts, 1)
            pool.wait_ge(consts, 1)
            link(nc.gpsimd.iota(iota_i[:, 0:P], [[1, P]], base=0, channel_multiplier=0))
            nc.gpsimd.tensor_copy(iotaL[:, :], iota_i[:, 0:P]).then_inc(consts, 1)
            pool.wait_ge(consts, 2)
            link(nc.gpsimd.iota(iota_i[:, 0:NT * WIN], [[1, NT * WIN]], base=1, channel_multiplier=0))
            nc.gpsimd.tensor_copy(iotaW[:, :], iota_i[:, 0:NT * WIN]).then_inc(consts, 1)
            pool.wait_ge(consts, 3)
            nc.gpsimd.memset(nhalf[:, :], -0.5).then_inc(consts, 1)
            nc.gpsimd.memset(ones_f[:, :], 1.0).then_inc(consts, 1)
            nc.gpsimd.memset(f(ones_r[:, :]), 1.0).then_inc(consts, 1)
            link(nc.gpsimd.memset(ident[:, :], 0.0))
            nc.gpsimd.affine_select(out=ident[:, :], in_=ident[:, :], compare_op=ALU.not_equal, fill=1.0, base=0,
                                    pattern=[[-1, P]], channel_multiplier=1).then_inc(consts, 1)
            link(nc.gpsimd.iota(iota_i[:, 0:NT * GRP], [[N, NT], [1, GRP]], base=0, channel_multiplier=0))
            nc.gpsimd.tensor_copy(iotaG[:, :, :].rearrange("p h d -> p (h d)"),
                                  iota_i[:, 0:NT * GRP]).then_inc(consts, 1)

            def norm(layer, t):
                pool.wait_ge(stats, layer * NT + t + 1)
                link(nc.gpsimd.tensor_scalar(var_e[:, layer, t:t + 1], mv[:, layer, t, 1:2], EPS, None, ALU.add))
                link(nc.gpsimd.tensor_tensor(rstd[:, layer, t:t + 1], var_e[:, layer, t:t + 1], nhalf[:, :], ALU.pow))
                nc.gpsimd.tensor_scalar(nmr[:, layer, t:t + 1], mv[:, layer, t, 0:1], rstd[:, layer, t:t + 1], -1.0,
                                        ALU.mult, ALU.mult).then_inc(normed, 1)

            def add_bv(t):
                pool.wait_ge(relu, t + 1)
                nc.gpsimd.tensor_tensor(xs[:, t, :], xs[:, t, :], bv_sb[:, :], ALU.add).then_inc(res_ready, 1)

            for t in range(NT):
                norm(0, t)
                if t == 0:
                    pool.wait_ge(ld_bv, 16)
                if t:
                    add_bv(t - 1)
            add_bv(NT - 1)
            pool.wait_ge(ld_b, 32)
            link(nc.gpsimd.tensor_scalar(b_sb[:, :], b_sb[:, :], alpha[:, :], None, ALU.mult))

            def fill(i):
                if i >= 2:
                    pool.wait_ge(pT_ps, 2 * (i - 1))
                nc.gpsimd.tensor_scalar(pr[i % 2][:, :], A_f[:, i, :], 0.0, negc[:, i:i + 1],
                                        ALU.mult, ALU.add).then_inc(filled, 1)

            pool.wait_ge(counts_final, 1)
            pool.wait_ge(proj_lo, NPROJ)
            pool.wait_ge(proj, NPROJ)
            fill(0)
            for i in range(1, NT + 2):
                if i < NT:
                    fill(i)
                if i >= 2:
                    norm(1, i - 2)
                    pool.wait_ge(relu, NT + i - 1)
                    link(nc.gpsimd.tensor_tensor(xs[:, i - 2, :], xs[:, i - 2, :], b_sb[:, :], ALU.add))
                    nc.gpsimd.tensor_tensor(xs[:, i - 2, :], xs[:, i - 2, :], h2f[i % 2][:, :],
                                            ALU.add).then_inc(res2_ready, 1)

        @block.scalar
        def _(act):
            act.dma_start(bqk[:, 0, :], bq_d).then_inc(ld_bqk, 16)
            act.dma_start(bqk[:, 1, :], bk_d).then_inc(ld_bqk, 16)
            act.dma_start(alpha[:, :], alpha_d.partition_broadcast(P)).then_inc(ld_b, 16)
            groups = [0]
            his = [0]

            def norm_relu(layer, t, out):
                act.wait_ge(normed, layer * NT + t + 1)
                nc.scalar.activation(out, xs[:, t, :], ACT.Relu, bias=nmr[:, layer, t:t + 1],
                                     scale=rstd[:, layer, t:t + 1]).then_inc(relu, 1)

            for step, n, *to in STEPS:
                if step == "splitw":
                    act.wait_ge(ld_wq, 16)
                    nc.scalar.activation(wq[0][:, :, :], wq_raw[:, :, :], ACT.Copy, scale=SCALE).then_inc(w_hi, 1)
                    act.wait_ge(ld_wk, 16)
                    nc.scalar.activation(wk[0][:, :, :], wk_raw[:, :, :], ACT.Copy).then_inc(w_hi, 1)
                elif step == "wv":
                    act.wait_ge(ld_wv, 16)
                    nc.scalar.activation(wv[0][:, :, :], wv_raw[:, :, :], ACT.Copy).then_inc(w_hi, 1)
                elif step == "ln":
                    norm_relu(0, n, h1[:, n, :])
                elif step == "T":
                    act.wait_ge(hT_ps, n + 1)
                    nc.scalar.activation(hT[0][:, :, n * P:(n + 1) * P],
                                         bank[6 + n % 2][:, :].rearrange("p (k c) -> p k c", k=KD),
                                         ACT.Copy).then_inc(hT_hi, 1)
                elif step == "count":
                    for g in range(NG):
                        if n <= LAST[g] // 2 < to[0]:
                            act.wait_ge(oh_used, LAST[g] // 2 + 1)
                            nc.scalar.activation(A[:, :, g * GRP:(g + 1) * GRP],
                                                 bank[g % 2][:, :].rearrange("p (h d) -> p h d", h=NT),
                                                 ACT.Copy).then_inc(count_kept, 1)
                elif step in ("M", "G", "V"):
                    i = proj_index((step, n))
                    ps = bank[2 + i % 4]
                    act.wait_ge(proj, i + 1)
                    if step == "M":
                        nc.scalar.activation(M[0][:, n, :], ps[:, :], ACT.Copy).then_inc(proj_hi, 1)
                    elif step == "G":
                        half, m = n // KD, n % KD
                        if n == 0:
                            act.wait_ge(proj_lo, proj_index(("vec", 0)) + 1)
                        nc.scalar.activation(GT[0][:, 4 * half:4 * half + 4, m, :],
                                             ps[:, :].rearrange("p (t c) -> p t c", t=4),
                                             ACT.Identity, bias=g0[:, m:m + 1]).then_inc(proj_hi, 1)
                    else:
                        nc.scalar.activation(V[0][:, n, :], ps[:, :], ACT.Copy).then_inc(proj_hi, 1)

            for i in range(NT + 2):
                if 1 <= i <= NT:
                    j = i - 1
                    if j >= 2:
                        act.wait_ge(attended, j - 1)
                    for q in range(2):
                        act.wait_ge(pT_ps, 2 * j + q + 1)
                        nc.scalar.activation(pT[j % 2][0][:, 4 * q:4 * q + 4, :],
                                             bank[q][:, :].rearrange("p (b c) -> p b c", b=4),
                                             ACT.Copy).then_inc(pT_hi, 1)
                if i < NT:
                    act.wait_ge(maxed, i + 1)
                    nc.scalar.activation(pr[i % 2][:, :], pr[i % 2][:, :], ACT.Exp, bias=negmax[:, i:i + 1],
                                         accum_out=rowsum[:, i:i + 1]).then_inc(expd, 1)
                if i == 3:
                    act.wait_ge(ld_wt, 16)
                    nc.scalar.activation(wt[0][:, :, :], wt_raw[:, :, :], ACT.Copy).then_inc(w_hi, 1)
                if i >= 2:
                    j = i - 2
                    if j >= 2:
                        act.wait_ge(h2_lo, j - 1)
                        act.wait_ge(res2_ready, j - 1)
                    norm_relu(1, j, h2f[j % 2][:, :])
                    act.wait_ge(relu, NT + j + 1)
                    nc.scalar.activation(h2[0][:, j, :], h2f[j % 2][:, :], ACT.Copy).then_inc(h2_hi, 1)

            for n in range(2 * KD):
                half, m = n // KD, n % KD
                act.wait_ge(agg_ps, n + 1)
                nc.scalar.activation(agT[0][:, m, half * HALF:(half + 1) * HALF], bank[AGG_BANK[n]][:, :],
                                     ACT.Copy).then_inc(agg_hi, 1)

        @block.vector
        def _(dve):
            chain = [0]

            def link(ins):
                chain[0] += 1
                ins.then_inc(dve_chain, 1)
                dve.wait_ge(dve_chain, chain[0])

            dve.wait_ge(ld_edges, 32)
            nc.vector.tensor_scalar(key_i[0][:, :], src_i[:, :], P - 1, None, ALU.bitwise_and)
            nc.vector.tensor_scalar(key_i[1][:, :], src_i[:, :], N - P, None, ALU.bitwise_and)
            dve.wait_ge(consts, 1)
            link(nc.vector.tensor_tensor(key_t[0][:, :], dst_i[:, :], win0[:, :], ALU.subtract))
            nc.vector.tensor_copy(lo_f[:, :], key_i[0][:, :])
            nc.vector.scalar_tensor_tensor(out=key_t[1][:, :], in0=key_i[1][:, :], scalar=float(WIN) / P,
                                           in1=key_t[0][:, :], op0=ALU.mult, op1=ALU.add)
            link(nc.vector.tensor_scalar(key_t[2][:, :], key_t[0][:, :], float(WIN), None, ALU.is_lt))
            link(nc.vector.scalar_tensor_tensor(out=key_t[3][:, :], in0=key_t[0][:, :], scalar=0.0,
                                                in1=key_t[2][:, :], op0=ALU.is_ge, op1=ALU.mult))
            link(nc.vector.scalar_tensor_tensor(out=key_f[:, :], in0=key_t[1][:, :], scalar=1.0,
                                                in1=key_t[3][:, :], op0=ALU.add, op1=ALU.mult))
            dve.wait_ge(consts, 3)

            def one_hots(a, b):
                for q in range(a, b):
                    if q >= RING:
                        dve.wait_ge(oh_used, q - RING + 1)
                    for u in range(2):
                        t = 2 * q + u
                        nc.vector.tensor_scalar(ohL[:, q % RING, u, :], iotaL[:, :], lo_f[:, t:t + 1], None, ALU.is_equal)
                        last = nc.vector.tensor_scalar(ohW[:, q % RING, u, :, :].rearrange("p h d -> p (h d)"),
                                                       iotaW[:, :], key_f[:, t:t + 1], None, ALU.is_equal)
                    last.then_inc(oh_ready, 1)

            def row_stats(layer, t):
                link(nc.vector.bn_stats(bn[:, layer, t, :], xs[:, t, :]))
                nc.vector.bn_aggr(mv[:, layer, t, :], bn[:, layer, t, :]).then_inc(stats, 1)

            def split_lo(k, hl, raw, scale=1.0):
                dve.wait_ge(w_hi, k + 1)
                nc.vector.scalar_tensor_tensor(out=hl[1][:, :, :], in0=raw[:, :, :], scalar=scale, in1=f(hl[0][:, :, :]),
                                               op0=ALU.mult, op1=ALU.subtract).then_inc(w_lo, 1)

            for step, n, *to in VSTEPS:
                if step == "splitw":
                    dve.wait_ge(ld_bqk, 32)
                    link(nc.vector.tensor_scalar(bqk[:, 0, :], bqk[:, 0, :], SCALE, None, ALU.mult))
                    nc.vector.tensor_tensor(bprod[:, :], bqk[:, 0, :], bqk[:, 1, :], ALU.mult)
                    nc.vector.tensor_copy(bqk_z[:, :, :, 0], bqk[:, :, :])
                    nc.vector.memset(f(bqk_z[:, :, :, 1]), 0.0)
                    link(nc.vector.tensor_copy(bqk_r[:, :, :, 0], bqk[:, :, :]))
                    nc.vector.tensor_tensor(bqk_r[:, :, :, 1], bqk[:, :, :], f(bqk_r[:, :, :, 0]),
                                            ALU.subtract).then_inc(vec_ready, 1)
                    one_hots(0, 4)
                    split_lo(0, wq, wq_raw, SCALE)
                    split_lo(1, wk, wk_raw)
                elif step == "count":
                    one_hots(max(n, 4), to[0])
                elif step == "wv":
                    dve.wait_ge(ld_wv, 16)
                    split_lo(2, wv, wv_raw)
                elif step == "ln":
                    if n % 2 == 0:
                        dve.wait_ge(ld_x[n // 2], 16)
                    row_stats(0, n)
                elif step == "T":
                    dve.wait_ge(hT_hi, n + 1)
                    hi = hT[0][:, :, n * P:(n + 1) * P]
                    nc.vector.tensor_tensor(hT[1][:, :, n * P:(n + 1) * P],
                                            bank[6 + n % 2][:, :].rearrange("p (k c) -> p k c", k=KD), f(hi),
                                            ALU.subtract).then_inc(hT_lo, 1)
                elif step == "vec":
                    i = proj_index((step, n))
                    ps = bank[2 + i % 4]
                    dve.wait_ge(proj, i + 1)
                    nc.vector.tensor_reduce(u_f[:, :], ps[:, 0:2 * KD].rearrange("p (m c) -> p m c", c=2), AX.X, ALU.add)
                    nc.vector.tensor_reduce(g0[:, :], ps[:, 2 * KD:4 * KD].rearrange("p (m c) -> p m c", c=2), AX.X, ALU.add)
                    nc.vector.memset(f(u_z[:, :, 1]), 0.0)
                    link(nc.vector.tensor_reduce(bb[:, :], ps[:, 4 * KD:5 * KD], AX.X, ALU.add))
                    nc.vector.tensor_copy(u_z[:, :, 0], u_f[:, :])
                    link(nc.vector.tensor_copy(u_r[:, :, 0], u_f[:, :]))
                    nc.vector.tensor_tensor(u_r[:, :, 1], u_f[:, :], f(u_r[:, :, 0]), ALU.subtract).then_inc(proj_lo, 1)
                elif step == "c":
                    i = proj_index((step, n))
                    dve.wait_ge(proj, i + 1)
                    link(nc.vector.tensor_reduce(c_f[:, :], bank[2 + i % 4][:, 0:2 * NT].rearrange("p (m c) -> p m c", c=2),
                                                 AX.X, ALU.add))
                    link(nc.vector.tensor_scalar(c_f[:, :], c_f[:, :], bb[:, :], None, ALU.add))
                    nc.vector.tensor_scalar(negc[:, :], c_f[:, :], -1.0, NEG, ALU.mult, ALU.add).then_inc(proj_lo, 1)
                else:
                    i = proj_index((step, n))
                    ps = bank[2 + i % 4]
                    dve.wait_ge(proj_hi, hi_before(i + 1))
                    if step == "M":
                        ins = nc.vector.tensor_tensor(M[1][:, n, :], ps[:, :], f(M[0][:, n, :]), ALU.subtract)
                    elif step == "G":
                        half, m = n // KD, n % KD
                        ins = nc.vector.scalar_tensor_tensor(
                            out=GT[1][:, 4 * half:4 * half + 4, m, :], in0=ps[:, :].rearrange("p (t c) -> p t c", t=4),
                            scalar=g0[:, m:m + 1], in1=f(GT[0][:, 4 * half:4 * half + 4, m, :]),
                            op0=ALU.add, op1=ALU.subtract)
                    else:
                        ins = nc.vector.tensor_tensor(V[1][:, n, :], ps[:, :], f(V[0][:, n, :]), ALU.subtract)
                    ins.then_inc(proj_lo, 1)

            dve.wait_ge(deg_ps, 1)
            deg_view = bank[0][:, 0:2 * NT].rearrange("p (j c) -> p j c", c=2)[:, :, 0]
            link(nc.vector.tensor_copy(deg[:, :], deg_view))
            nc.vector.tensor_reduce(stat[:, 0:1], deg[:, :], AX.X, ALU.add)
            link(nc.vector.tensor_reduce(dmax[:, :], deg[:, :], AX.X, ALU.max))
            nc.vector.tensor_scalar(stat[:, 1:2], dmax[:, :], float(EXACT), None, ALU.is_ge).then_inc(stat_ready, 1)
            dve.wait_ge(stat_ps, 1)
            link(nc.vector.tensor_copy(found[0:1, :], bank[1][0:1, 0:2]))
            link(nc.vector.tensor_scalar(stat[0:1, 0:1], found[0:1, 0:1], float(E), None, ALU.not_equal))
            nc.vector.tensor_tensor(flag[0:1, :], stat[0:1, 0:1], found[0:1, 1:2], ALU.add).then_inc(flag_ready, 1)
            dve.wait_ge(flag_ready, 1)
            general = nc.vector.value_load(flag[0:1, 0:1], min_val=0, max_val=P + 1)
            with dve.If(general > 0):
                nc.vector.memset(gen0[:, :], 0.0)
                nc.vector.tensor_scalar(gen_i[:, :], src_i[:, :], N - P, None, ALU.bitwise_and).then_inc(gen_prep, 1)
                dve.wait_ge(gen_prep, 1)
                nc.vector.scalar_tensor_tensor(out=gen_key[:, :], in0=gen_i[:, :], scalar=float(N) / P, in1=dst_i[:, :],
                                               op0=ALU.mult, op1=ALU.add).then_inc(gen_prep, 1)
                nc.vector.memset(dmax[:, :], 0.0).then_inc(gen_R_s, 1)
                dve.wait_ge(gen_prep, 2)
                dve.wait_ge(consts, 8)
                with dve.Fori(0, NG) as g:
                    with dve.Fori(0, PAIRS) as q:
                        dve.wait_ge(gen_used, g * PAIRS + q + 1)
                        for u in range(2):
                            nc.vector.tensor_scalar(genL[:, u, :], iotaL[:, :], lo_f[:, bass.ds(2 * q + u, 1)], None,
                                                    ALU.is_equal)
                            last = nc.vector.tensor_scalar(genW[:, u, :], iotaG[:, :, :].rearrange("p h d -> p (h d)"),
                                                           gen_key[:, bass.ds(2 * q + u, 1)], None, ALU.is_equal)
                        last.then_inc(gen_ready, 1)
                    nc.vector.tensor_scalar(iotaG[:, :, :], iotaG[:, :, :], float(GRP), None, ALU.add).then_inc(gen_iota, 1)
                    dve.wait_ge(gen_ps, g + 1)
                    got = bank[0][:, :].rearrange("p (h d) -> p h d", h=NT)
                    nc.vector.tensor_copy(A[:, :, bass.ds(g * GRP, GRP)], got).then_inc(gen_A, 1)
                    dve.wait_ge(gen_A, g + 1)
                    nc.vector.tensor_tensor(R[:, :, bass.ds(g * GRP, GRP)], got, A_f[:, :, bass.ds(g * GRP, GRP)],
                                            ALU.subtract).then_inc(gen_R_s, 1)
                    dve.wait_ge(gen_iota, g + 1)
                    dve.wait_ge(gen_R_s, g + 2)
                for h in range(NT):
                    if h:
                        dve.wait_ge(gen_deg, h)
                    nc.vector.tensor_copy(gen_R[:, :], R[:, h, :]).then_inc(gen_stage, 1)
                dve.wait_ge(gen_deg, NT)
                nc.vector.tensor_copy(deg[:, :], deg_view)
            nc.vector.memset(dmax[:, :], 0.0).then_inc(counts_final, 1)
            dve.wait_ge(counts_final, 1)
            link(nc.vector.tensor_scalar(deg[:, :], deg[:, :], 1.0, None, ALU.max))
            link(nc.vector.reciprocal(rdeg[:, :], deg[:, :]))
            dve.wait_ge(ld_b, 32)
            nc.vector.tensor_scalar(rdeg[:, :], rdeg[:, :], alpha[:, :], None, ALU.mult).then_inc(rdeg_ready, 1)

            def h2_lo_part(j):
                dve.wait_ge(h2_hi, j + 1)
                nc.vector.tensor_tensor(h2[1][:, j, :], h2f[j % 2][:, :], f(h2[0][:, j, :]), ALU.subtract).then_inc(h2_lo, 1)

            for i in range(NT + 2):
                if i >= 3:
                    h2_lo_part(i - 3)
                if i < NT:
                    dve.wait_ge(filled, i + 1)
                    for q in range(2):
                        dve.wait_ge(scored, 2 * i + q + 1)
                        cols = slice(q * HALF, (q + 1) * HALF)
                        ins = nc.vector.copy_predicated(pr[i % 2][:, cols], A_i[:, i, cols], bank[2 + (2 * i + q) % 4][:, :])
                        ins.then_inc(masked, 1)
                    dve.wait_ge(masked, 2 * i + 2)
                    nc.vector.tensor_reduce(negmax[:, i:i + 1], pr[i % 2][:, :], AX.X, ALU.max, negate=True).then_inc(maxed, 1)
                if i == 3:
                    dve.wait_ge(ld_wt, 16)
                    split_lo(3, wt, wt_raw)
                if 1 <= i <= NT:
                    j = i - 1
                    for q in range(2):
                        dve.wait_ge(pT_hi, 2 * j + q + 1)
                        nc.vector.tensor_tensor(pT[j % 2][1][:, 4 * q:4 * q + 4, :],
                                                bank[q][:, :].rearrange("p (b c) -> p b c", b=4),
                                                f(pT[j % 2][0][:, 4 * q:4 * q + 4, :]), ALU.subtract).then_inc(pT_lo, 1)
                if i >= 2:
                    j = i - 2
                    dve.wait_ge(expd, j + 1)
                    link(nc.vector.reciprocal(rinv[:, j:j + 1], rowsum[:, j:j + 1]))
                    dve.wait_ge(attended, j + 1)
                    nc.vector.scalar_tensor_tensor(out=xs[:, j, :], in0=bank[6 + j % 2][:, :], scalar=rinv[:, j:j + 1],
                                                   in1=xs[:, j, :], op0=ALU.mult, op1=ALU.add).then_inc(x2_ready, 1)
                    dve.wait_ge(x2_ready, j + 1)
                    row_stats(1, j)
            h2_lo_part(NT - 1)

            with dve.If(general > 0):
                for k in range(2 * NT):
                    half, h = k // NT, k % NT
                    if k == 0:
                        dve.wait_ge(h2_lo, NT)
                        dve.wait_ge(res2_ready, NT)
                    if k >= 2:
                        dve.wait_ge(agg_used, k - 1)
                    nc.vector.tensor_copy(r_st[k % 2][:, :], R[:, h, half * HALF:(half + 1) * HALF]).then_inc(agg_stage, 1)

            for n in range(2 * KD):
                half, m = n // KD, n % KD
                cols = slice(half * HALF, (half + 1) * HALF)
                dve.wait_ge(agg_hi, n + 1)
                nc.vector.tensor_tensor(agT[1][:, m, cols], bank[AGG_BANK[n]][:, :], f(agT[0][:, m, cols]),
                                        ALU.subtract).then_inc(agg_lo, 1)
            dve.wait_ge(rdeg_ready, 1)
            for j in range(NT):
                dve.wait_ge(res2_ready, j + 1)
                dve.wait_ge(out_ps, j + 1)
                nc.vector.scalar_tensor_tensor(out=o_sb[:, j, :], in0=bank[2 + j % 4][:, :], scalar=rdeg[:, j:j + 1],
                                               in1=xs[:, j, :], op0=ALU.mult, op1=ALU.add).then_inc(out_ready, 1)

        @block.tensor
        def _(pe):
            mm = nc.tensor.matmul

            def three_pass(out, lhs, rhs, pairs):
                for k, (a, b) in enumerate(pairs):
                    mm(out, lhs[0][a], rhs[0][b], start=(k == 0), stop=False)
                    mm(out, lhs[0][a], rhs[1][b], start=False, stop=False)
                    last = mm(out, lhs[1][a], rhs[0][b], start=False, stop=(k == len(pairs) - 1))
                return last

            def vector_product(out, lhs, v_r, v_z, pairs):
                for k, (a, b) in enumerate(pairs):
                    mm(out, lhs[0][a], v_r[b], start=(k == 0), stop=False)
                    last = mm(out, lhs[1][a], v_z[b], start=False, stop=(k == len(pairs) - 1))
                return last

            def count(a, b):
                for q in range(a, b):
                    pe.wait_ge(oh_ready, q + 1)
                    for u in range(2):
                        t = 2 * q + u
                        w = window(t)
                        for g, c0, c1 in pieces(t):
                            if FIRST[g] == t and g >= 2:
                                pe.wait_ge(count_kept, g - 1)
                            out = bank[g % 2][:, :].rearrange("p (h d) -> p h d", h=NT)[:, :, c0 - g * GRP:c1 - g * GRP]
                            last = mm(out, ohL[:, q % RING, u, :], ohW[:, q % RING, u, :, c0 - w:c1 - w],
                                      start=(FIRST[g] == t), stop=(LAST[g] == t), skip_group_check=True)
                    last.then_inc(oh_used, 1)

            def sl(*ix):
                return tuple(slice(i * P, (i + 1) * P) if isinstance(i, int) else i for i in ix)

            every = slice(None)

            def cols(k, m, width=P):
                return (every, k, slice(m * width, (m + 1) * width))

            for step, n, *to in STEPS:
                if step == "count":
                    count(n, to[0])
                elif step == "T":
                    if n == 0:
                        pe.wait_ge(consts, 7)
                    pe.wait_ge(relu, n + 1)
                    if n >= 2:
                        pe.wait_ge(hT_lo, n - 1)
                    for k in range(KD):
                        last = nc.tensor.transpose(bank[6 + n % 2][:, k * P:(k + 1) * P], h1[:, n, k * P:(k + 1) * P],
                                                   ident[:, :])
                    last.then_inc(hT_ps, 1)
                elif step in ("M", "vec", "G", "c", "V"):
                    i = proj_index((step, n))
                    ps = bank[2 + i % 4]
                    if i >= 4:
                        pe.wait_ge(proj_lo, i - 3)
                    if step == "M":
                        if n == 0:
                            pe.wait_ge(w_lo, 2)
                        last = three_pass(ps[:, :], wq, wk, [(cols(k, n), cols(k, 0, D)) for k in range(KD)])
                    elif step == "vec":
                        pe.wait_ge(vec_ready, 1)
                        for m in range(KD):
                            vector_product(ps[:, 2 * m:2 * m + 2], wq, bqk_r, bqk_z,
                                           [(cols(k, m), (every, 1, k, every)) for k in range(KD)])
                        for m in range(KD):
                            o = 2 * KD + 2 * m
                            vector_product(ps[:, o:o + 2], wk, bqk_r, bqk_z,
                                           [(cols(k, m), (every, 0, k, every)) for k in range(KD)])
                        last = mm(ps[:, 4 * KD:5 * KD], ones_f[:, :], bprod[:, :], start=True, stop=True)
                    elif step == "G":
                        half, m = n // KD, n % KD
                        if m == 0:
                            pe.wait_ge(hT_lo, 4 * (half + 1))
                            pe.wait_ge(proj_lo, KD)
                        last = three_pass(ps[:, :], M, hT, [(cols(k, m), cols(k, half, HALF)) for k in range(KD)])
                    elif step == "c":
                        pe.wait_ge(proj_lo, proj_index(("vec", 0)) + 1)
                        for t in range(NT):
                            last = vector_product(ps[:, 2 * t:2 * t + 2], hT, u_r, u_z,
                                                  [(cols(k, t), (every, k, every)) for k in range(KD)])
                    else:
                        if n == 0:
                            pe.wait_ge(w_lo, 3)
                        last = three_pass(ps[:, :], hT, wv, [(cols(k, n), cols(k, 0, D)) for k in range(KD)])
                    last.then_inc(proj, 1)

            def scores(i):
                for q in range(2):
                    if i < 2:
                        pe.wait_ge(proj_lo, NPROJ)
                    else:
                        pe.wait_ge(masked, 2 * (i - 2) + q + 1)
                    three_pass(bank[2 + (2 * i + q) % 4][:, :], GT, hT,
                               [((every, i, k, every), cols(k, q, HALF)) for k in range(KD)]).then_inc(scored, 1)

            def degrees(rows, first, stop):
                for j in range(NT):
                    for n, row in enumerate(rows):
                        last = mm(bank[0][:, 2 * j:2 * j + 2], row[:, j * P:(j + 1) * P], ones_r[:, :],
                                  start=(first and j == 0 and n == 0), stop=stop and n == len(rows) - 1,
                                  skip_group_check=True)
                return last

            scores(0)
            pe.wait_ge(count_kept, NG)
            degrees([A[:, h, :] for h in range(NT)], True, True).then_inc(deg_ps, 1)
            scores(1)
            pe.wait_ge(stat_ready, 1)
            mm(bank[1][0:1, 0:2], ones_f[:, 0:1], stat[:, :], start=True, stop=True).then_inc(stat_ps, 1)
            pe.wait_ge(flag_ready, 1)
            general = nc.tensor.value_load(flag[0:1, 0:1], min_val=0, max_val=P + 1)
            with pe.If(general > 0):
                pe.wait_ge(gen_prep, 2)
                mm(bank[0][:, 0:P], gen0[:, 0:P], gen0[:, 0:P], start=True, stop=True).then_inc(gen_used, 1)
                with pe.Fori(0, NG) as g:
                    pe.wait_ge(gen_R_s, g + 1)
                    mm(bank[0][:, :], gen0[:, 0:P], gen0[:, :], start=True, stop=False, skip_group_check=True)
                    with pe.Fori(0, PAIRS) as q:
                        pe.wait_ge(gen_ready, g * PAIRS + q + 1)
                        for u in range(2):
                            last = mm(bank[0][:, :], genL[:, u, :], genW[:, u, :], start=False, stop=False,
                                      skip_group_check=True)
                        last.then_inc(gen_used, 1)
                    mm(bank[0][:, :], gen0[:, 0:P], gen0[:, :], start=False, stop=True,
                       skip_group_check=True).then_inc(gen_ps, 1)
                pe.wait_ge(gen_R_s, NG + 1)
                degrees([A[:, h, :] for h in range(NT)], True, False)
                for h in range(NT):
                    pe.wait_ge(gen_stage, h + 1)
                    degrees([gen_R[:, :]], False, h == NT - 1).then_inc(gen_deg, 1)

            for i in range(NT + 2):
                if 2 <= i < NT:
                    scores(i)
                if 1 <= i <= NT:
                    j = i - 1
                    pe.wait_ge(expd, j + 1)
                    if j == 0:
                        pe.wait_ge(counts_final, 1)
                    for q in range(2):
                        if j >= 1:
                            pe.wait_ge(pT_lo, 2 * (j - 1) + q + 1)
                        for b in range(4):
                            c = (4 * q + b) * P
                            last = nc.tensor.transpose(bank[q][:, b * P:(b + 1) * P], pr[j % 2][:, c:c + P], ident[:, :])
                        last.then_inc(pT_ps, 1)
                if i >= 2:
                    j = i - 2
                    pe.wait_ge(pT_lo, 2 * (j + 1))
                    if j >= 2:
                        pe.wait_ge(x2_ready, j - 1)
                    if i == NT + 1:
                        aggregate(nc, pe, mm, bank, h2, A, range(0, NT - 2), range(0, KD), masked, h2_lo)
                    three_pass(bank[6 + j % 2][:, :], pT[j % 2], V,
                               [((every, b, every), (every, b, every)) for b in range(NT)]).then_inc(attended, 1)

            pe.wait_ge(h2_lo, NT - 1)
            aggregate(nc, pe, mm, bank, h2, A, range(NT - 2, NT - 1), range(0, KD), None, None)
            pe.wait_ge(pT_lo, 2 * NT)
            pe.wait_ge(x2_ready, NT)
            aggregate(nc, pe, mm, bank, h2, A, range(0, NT - 1), range(KD, 2 * KD), None, None)
            pe.wait_ge(h2_lo, NT)
            with pe.If(general > 0):
                for k in range(2 * NT):
                    half, h = k // NT, k % NT
                    pe.wait_ge(agg_stage, k + 1)
                    for m in range(KD):
                        for hl in range(2):
                            last = mm(bank[AGG_BANK[half * KD + m]][:, :], h2[hl][:, h, m * P:(m + 1) * P],
                                      r_st[k % 2][:, :], start=False, stop=False, skip_group_check=True)
                    last.then_inc(agg_used, 1)
            for n in range(2 * KD):
                half, m = n // KD, n % KD
                for hl in range(2):
                    last = mm(bank[AGG_BANK[n]][:, :], h2[hl][:, NT - 1, m * P:(m + 1) * P],
                              A[:, NT - 1, half * HALF:(half + 1) * HALF], start=False, stop=(hl == 1),
                              skip_group_check=True)
                last.then_inc(agg_ps, 1)

            pe.wait_ge(w_lo, 4)
            for j in range(NT):
                if j % 4 == 0:
                    pe.wait_ge(agg_lo, KD * (j // 4 + 1))
                if j >= 4:
                    pe.wait_ge(out_ready, j - 3)
                three_pass(bank[2 + j % 4][:, :], agT, wt,
                           [(cols(k, j), cols(k, 0, D)) for k in range(KD)]).then_inc(out_ps, 1)


AGG_BANK = [2, 3, 4, 5, 0, 1, 6, 7]


def aggregate(nc, pe, mm, bank, h2, A, rows, groups, masked, h2_lo):
    for h in rows:
        if masked is not None:
            if h == 0:
                pe.wait_ge(masked, 2 * NT)
            pe.wait_ge(h2_lo, h + 1)
        for n in groups:
            half, m = n // KD, n % KD
            for hl in range(2):
                mm(bank[AGG_BANK[n]][:, :], h2[hl][:, h, m * P:(m + 1) * P], A[:, h, half * HALF:(half + 1) * HALF],
                   start=(h == 0 and hl == 0), stop=False, skip_group_check=True)


def kernel(**inputs):
    import numpy as _np
    import concourse.bacc as _bacc
    from concourse import mybir as _mybir
    from concourse.bass_utils import run_bass_kernel_spmd as _run

    def columns(v):
        return _np.asarray(v).reshape(-1, P).T

    layout = {
        "x": _np.asarray(inputs["x"]),
        "src": columns(inputs["src"]), "dst": columns(inputs["dst"]),
        "wqT": _np.asarray(inputs["L0_gnn_Wq"]).T, "wkT": _np.asarray(inputs["L0_gnn_Wk"]).T,
        "wv": _np.asarray(inputs["L0_gnn_Wv"]), "wT": _np.asarray(inputs["L1_gnn_W"]).T,
        "bq": columns(inputs["L0_gnn_bq"]), "bk": columns(inputs["L0_gnn_bk"]),
        "bv": _np.asarray(inputs["L0_gnn_bv"]), "b": _np.asarray(inputs["L1_gnn_b"]),
        "alpha": _np.asarray(inputs["L1_gnn_alpha"]).reshape(1),
    }
    nc = _bacc.Bacc("TRN2", target_bir_lowering=False, num_devices=1)
    arrays, args = {}, []
    for name, a in layout.items():
        a = _np.ascontiguousarray(a)
        arrays[f"in_{name}"] = a
        args.append(nc.dram_tensor(f"in_{name}", a.shape, _mybir.dt.from_np(a.dtype), kind="ExternalInput").ap())
    out = nc.dram_tensor("out_dram", (N, D), _mybir.dt.float32, kind="ExternalOutput").ap()
    gnn_kernel(nc, *args, out)
    r = _run(nc, [arrays], core_ids=[0])
    return r.results[0]["out_dram"]
```

```python
import concourse.bass as bass
from concourse import mybir
from contextlib import ExitStack

F32 = mybir.dt.float32
F32R = mybir.dt.float32r
BF16 = mybir.dt.bfloat16
I32 = mybir.dt.int32
I8 = mybir.dt.int8
ALU = mybir.AluOpType
ACT = mybir.ActivationFunctionType
AX = mybir.AxisListType

P = 128
N, D, E = 1024, 512, 33792
NT = N // P
KD = D // P
ET = E // P
HALF = N // 2
NEG = -1.0e6
EPS = 1e-5
SCALE = 1.0 / float(D) ** 0.5

WIN = 32
GRP = 64
NG = N // GRP
TPB = 33
WSTEP, WBACK = 4, 16
EXACT = 4096

BATCH = 4
NB = ET // BATCH
RING = 4


def window(t):
    return min(max(P * (t // TPB) + WSTEP * (t % TPB) - WBACK, 0), N - WIN)


def pieces(t):
    w = window(t)
    return [(g, max(w, GRP * g), min(w + WIN, GRP * g + GRP)) for g in range(w // GRP, (w + WIN - 1) // GRP + 1)]


FIRST = {g: min(t for t in range(ET) if any(p[0] == g for p in pieces(t))) for g in range(NG)}
LAST = {g: max(t for t in range(ET) if any(p[0] == g for p in pieces(t))) for g in range(NG)}


def schedule():
    heavy = [("M", m) for m in range(KD)] + [("u", 0), ("g", 0)]
    heavy += [("G", n) for n in range(2 * KD)] + [("V", t) for t in range(NT)]
    batches = {"M": 3, "u": 3, "g": 3, "G": 2, "V": 3}
    groups, at, rounds = [[("splitw", 0)]], 0, 0

    def norms(group):
        nonlocal rounds
        group += [(what, rounds - lag) for lag, what in enumerate(("sum", "squares", "rows")) if 0 <= rounds - lag < NT]
        rounds += 1

    def count(group, n):
        nonlocal at
        if at < NB:
            group.append(("count", at, min(at + n, NB)))
            at = min(at + n, NB)

    count(groups[0], START)
    groups.append([])
    for _ in range(3):
        norms(groups[-1])
    groups[-1].append(("Ma", 0))
    count(groups[-1], RING)
    for j, s in enumerate(heavy):
        group = []
        norms(group)
        if s[0] == "G":
            group.append(("c", s[1]))
        if s in (("G", 2), ("G", 3)):
            group.append(("wv", s[1] - 2))
        group.append(s)
        if j < NT:
            group.append(("T", j))
        count(group, batches[s[0]])
        groups.append(group)
    while at < NB:
        groups.append([])
        count(groups[-1], 3)
    return groups


START = 3
GROUPS = schedule()
STEPS = [s for group in GROUPS for s in group]
VSTEPS = [s for group in GROUPS[:1] for s in group]
VSTEPS += [s for group in GROUPS[1:] for s in sorted(group, key=lambda s: s[0] != "count")]
PROJ = [s for s in STEPS if s[0] in ("M", "u", "g", "G", "V")]
NPROJ = len(PROJ)


def hi_before(n):
    return sum(s[0] in ("M", "u", "G", "V") for s in PROJ[:n])


def gnn_kernel(nc, x_d, src_d, dst_d, wqT_d, wkT_d, wv_d, wT_d, bq_d, bk_d, bv_d, b_d, alpha_d, out_d):
    with ExitStack() as ctx:
        base = ctx.enter_context(nc.sbuf_tensor("arena", [P, 53150], F32))
        top = nc.sbuf_base
        start = top - 53150 * 4
        at = [start + (-start) % 32]

        def region(nbytes):
            a = at[0]
            at[0] += (nbytes + 31) // 32 * 32
            assert at[0] <= top, (at[0], top)
            return a

        def place(name, shape, dt, offset):
            return nc.alloc_sbuf_tensor_at(name, shape, dt, offset=offset)

        def small(name, shape, dt):
            size = 2 if dt == BF16 else 4
            for s in shape[1:]:
                size *= s
            return place(name, shape, dt, region(size))

        KB = 1024
        r_hT, r_G, r_V, r_A = (region(32 * KB) for _ in range(4))
        r_x, r_W0, r_W2, r_W1, r_R = region(16 * KB), region(16 * KB), region(16 * KB), region(16 * KB), region(8 * KB)

        hT = [place("hT_hi", [P, KD, N], F32R, r_hT), place("hT_lo", [P, KD, N], F32R, r_hT + 16 * KB)]
        agT = [place("agT_hi", [P, KD, N], F32R, r_hT), place("agT_lo", [P, KD, N], F32R, r_hT + 16 * KB)]
        GT = [place("GT_hi", [P, NT, KD, P], F32R, r_G), place("GT_lo", [P, NT, KD, P], F32R, r_G + 16 * KB)]
        h2 = [place("h2_hi", [P, NT, D], F32R, r_G), place("h2_lo", [P, NT, D], F32R, r_G + 16 * KB)]
        iota_i = place("iota_i", [P, NT * GRP], I32, r_G)
        win_i = place("win_i", [P, ET], I32, r_G + 2 * KB)
        win0 = place("win0", [P, ET], F32, r_G + 4 * KB)
        key_t = [place(f"key_t{i}", [P, ET], F32, r_G + (6 + 2 * i) * KB) for i in range(4)]
        key_i = [place(f"key_i{i}", [P, ET], I32, r_G + (14 + 2 * i) * KB) for i in range(2)]
        b_rep = [place("b_rep_hi", [P, 2, KD, P], F32R, r_G + 18 * KB),
                 place("b_rep_lo", [P, 2, KD, P], F32R, r_G + 22 * KB)]
        V = [place("V_hi", [P, NT, D], F32R, r_V), place("V_lo", [P, NT, D], F32R, r_V + 16 * KB)]
        h1 = place("h1", [P, NT, D], F32, r_V)
        wk = [place("wk_hi", [P, KD, D], F32R, r_V + 16 * KB), place("wk_lo", [P, KD, D], F32R, r_V + 24 * KB)]
        wk_raw = place("wk_raw", [P, KD, D], F32, r_V + 24 * KB)
        o_sb = place("o_sb", [P, NT, D], F32, r_V)
        A = place("A", [P, NT, N], F32R, r_A)
        A_f = A[:, :, :].bitcast(F32)
        A_i = A[:, :, :].bitcast(I32)
        R = place("R", [P, NT, N], I8, r_R)
        bv_sb, u_sb, uh = (place(n, [P, D], F32, r_R + 2 * KB * i) for i, n in enumerate(("bv_sb", "u_sb", "uh")))
        diag_g = place("diag_g", [P, P], BF16, r_R + 6 * KB)
        xs = place("xs", [P, NT, D], F32, r_x)
        wq = [place("wq_hi", [P, KD, D], F32R, r_W0), place("wq_lo", [P, KD, D], F32R, r_W0 + 8 * KB)]
        wq_raw = place("wq_raw", [P, KD, D], F32, r_W0 + 8 * KB)
        wv = [place("wv_hi", [P, KD, D], F32R, r_W0), place("wv_lo", [P, KD, D], F32R, r_W0 + 8 * KB)]
        wv_raw = place("wv_raw", [P, KD, D], F32, r_W0 + 8 * KB)
        M = [place("M_hi", [P, KD, D], F32R, r_W2), place("M_lo", [P, KD, D], F32R, r_W2 + 8 * KB)]
        pr = [place(f"pr{i}", [P, N], F32, r_W0 + 4 * KB * i) for i in range(2)]
        pT = [[place(f"pT_hi{i}", [P, NT, P], F32R, r_W0 + (8 + 8 * i) * KB),
               place(f"pT_lo{i}", [P, NT, P], F32R, r_W0 + (12 + 8 * i) * KB)] for i in range(2)]
        h2f = [place(f"h2f{i}", [P, D], F32, r_W0 + (24 + 2 * i) * KB) for i in range(2)]
        r_st = [place(f"r_st{i}", [P, HALF], F32R, r_W0 + (24 + 2 * i) * KB) for i in range(2)]
        b_sb = place("b_sb", [P, D], F32, r_W0 + 28 * KB)
        diag_d = place("diag_d", [P, P], BF16, r_W0 + 30 * KB)
        ohL = place("ohL", [P, RING, P, BATCH], BF16, r_W1)
        ohW = place("ohW", [P, RING, NT, WIN, BATCH], BF16, r_W1 + RING * BATCH * P * 2)
        iotaG = place("iotaG", [P, NT, GRP], F32, r_W1 + 13 * KB)
        iotaL = place("iotaL", [P, P, BATCH], BF16, r_W1 + 15 * KB)
        dcopy = place("dcopy", [P, N], F32, r_W1)
        genL = place("genL", [P, 2, P], BF16, r_W1)
        genW = place("genW", [P, 2, NT * GRP], BF16, r_W1 + 1 * KB)
        gen0 = place("gen0", [P, NT * GRP], BF16, r_W1 + 3 * KB)
        gen_key = place("gen_key", [P, ET], F32, r_W1 + 4 * KB)
        gen_i = place("gen_i", [P, ET], I32, r_W1 + 6 * KB)
        gen_lo = place("gen_lo", [P, ET], F32, r_W1 + 8 * KB)
        gen_R = place("gen_R", [P, N], F32R, r_W1 + 6 * KB)
        wt = [place("wt_hi", [P, KD, D], F32R, r_W1), place("wt_lo", [P, KD, D], F32R, r_W1 + 8 * KB)]
        wt_raw = place("wt_raw", [P, KD, D], F32, r_W1 + 8 * KB)

        src_i, dst_i = small("src_i", [P, ET], I32), small("dst_i", [P, ET], I32)
        lo_b, key_b = small("lo_b", [P, ET], BF16), small("key_b", [P, ET], BF16)
        iotaW = small("iotaW", [P, NT * WIN, BATCH], BF16)
        ident, ones_r = small("ident", [P, P], F32), small("ones_r", [P, P], F32R)
        bqk = small("bqk", [P, 2, KD], F32)
        bprod, g0 = small("bprod", [P, KD], F32), small("g0", [P, KD], F32)
        bb, c_f, negc = small("bb", [P, 1], F32), small("c_f", [P, NT], F32), small("negc", [P, NT], F32)
        bn = small("bn", [P, NT, 6], F32)
        mv = small("mv", [P, NT, 2], F32)
        xsum, xsq, nmean = (small(n, [P, NT], F32) for n in ("xsum", "xsq", "nmean"))
        nhalf = small("nhalf", [P, 1], F32)
        var_e, rstd, nmr = (small(n, [P, 2, NT], F32) for n in ("var_e", "rstd", "nmr"))
        negmax, rowsum, rinv = (small(n, [P, NT], F32) for n in ("negmax", "rowsum", "rinv"))
        deg, rdeg = small("deg", [P, NT], F32), small("rdeg", [P, NT], F32)
        alpha = small("alpha", [P, 1], F32)
        dsum, dmax, dbad = small("dsum", [P, 2], F32), small("dmax", [P, 2], F32), small("dbad", [P, 2], F32)
        flag = small("flag", [P, 1], I32)

        bank = [ctx.enter_context(nc.psum_tensor(f"bank{i}", [P, 512], F32)) for i in range(8)]

        def sem(name):
            return ctx.enter_context(nc.semaphore(name))

        ld_edges, ld_wv, ld_wt = (sem(n) for n in ("ld_edges", "ld_wv", "ld_wt"))
        ld_wq, ld_wk = ([sem(f"{n}{q}") for q in range(2)] for n in ("ld_wq", "ld_wk"))
        ld_x = [sem(f"ld_x{i}") for i in range(4)]
        ld_bqk, ld_bv, ld_b, stored = sem("ld_bqk"), sem("ld_bv"), sem("ld_b"), sem("stored")
        consts = sem("consts")
        tables = sem("tables")
        pool_chain, dve_chain = sem("pool_chain"), sem("dve_chain")
        oh_ready, oh_used = sem("oh_ready"), sem("oh_used")
        count_kept = sem("count_kept")
        w_hi, w_lo = sem("w_hi"), sem("w_lo")
        vec_ready = sem("vec_ready")
        summed, centred, squared, stats = sem("summed"), sem("centred"), sem("squared"), sem("stats")
        normed, relu = sem("normed"), sem("relu")
        hT_ps, hT_hi, hT_lo = sem("hT_ps"), sem("hT_hi"), sem("hT_lo")
        proj, proj_hi, proj_lo = sem("proj"), sem("proj_hi"), sem("proj_lo")
        res_ready = sem("res_ready")
        bb_ps, bb_kept, c_ready = sem("bb_ps"), sem("bb_kept"), sem("c_ready")
        deg_sum = sem("deg_sum")
        deg_ps, deg_kept, flag_ready = sem("deg_ps"), sem("deg_kept"), sem("flag_ready")
        counts_final = sem("counts_final")
        gen_ready, gen_used, gen_ps, gen_A, gen_R_s = (sem(n) for n in ("gen_ready", "gen_used", "gen_ps", "gen_A", "gen_R_s"))
        gen_prep, gen_iota, gen_stage, gen_deg = (sem(n) for n in ("gen_prep", "gen_iota", "gen_stage", "gen_deg"))
        agg_stage, agg_used = sem("agg_stage"), sem("agg_used")
        filled, scored, masked, maxed, expd = (sem(n) for n in ("filled", "scored", "masked", "maxed", "expd"))
        pT_ps, pT_hi, pT_lo = sem("pT_ps"), sem("pT_hi"), sem("pT_lo")
        attended, x2_ready, h2_hi, h2_lo, res2_ready = (sem(n) for n in ("attended", "x2_ready", "h2_hi", "h2_lo", "res2_ready"))
        agg_ps, agg_hi, agg_lo = sem("agg_ps"), sem("agg_hi"), sem("agg_lo")
        rdeg_ready, out_ps, out_ready = sem("rdeg_ready"), sem("out_ps"), sem("out_ready")

        def part(T, hl, *ix):
            return T[hl].__getitem__(ix)

        def f(ap):
            return ap.bitcast(F32)

        def bcast(ap, dim, n):
            return ap.unsqueeze(dim).broadcast_to([*ap.shape[:dim], n, *ap.shape[dim:]])

        def proj_index(step):
            return PROJ.index(step)

        block = ctx.enter_context(nc.Block())

        @block.sync
        def _(sp):
            sp.dma_start(dst_i[:, :], dst_d).then_inc(ld_edges, 16)
            sp.dma_start(src_i[:, :], src_d).then_inc(ld_edges, 16)
            for q in range(2):
                for raw, w_d, loaded in ((wq_raw, wqT_d, ld_wq), (wk_raw, wkT_d, ld_wk)):
                    sp.dma_start(raw[:, 2 * q:2 * q + 2, :],
                                 w_d[2 * q * P:(2 * q + 2) * P, :].rearrange("(k p) n -> p k n", p=P)).then_inc(loaded[q], 16)
            for i in range(4):
                sp.dma_start(xs[:, 2 * i:2 * i + 2, :],
                             x_d[2 * i * P:(2 * i + 2) * P, :].rearrange("(t p) n -> p t n", p=P)).then_inc(ld_x[i], 16)
            sp.dma_start(bv_sb[:, :], bv_d.partition_broadcast(P)).then_inc(ld_bv, 16)
            sp.wait_ge(proj, proj_index(("u", 0)) + 1)
            sp.dma_start(wv_raw[:, :, :], wv_d.rearrange("(k p) n -> p k n", p=P)).then_inc(ld_wv, 16)
            sp.wait_ge(proj, NPROJ)
            sp.dma_start(b_sb[:, :], b_d.partition_broadcast(P)).then_inc(ld_b, 16)
            sp.wait_ge(counts_final, 1)
            sp.wait_ge(res_ready, NT)
            sp.dma_start(wt_raw[:, :, :], wT_d.rearrange("(k p) n -> p k n", p=P)).then_inc(ld_wt, 16)
            for j in range(NT):
                sp.wait_ge(out_ready, j + 1)
                sp.dma_start(out_d[j * P:(j + 1) * P, :], o_sb[:, j, :]).then_inc(stored, 16)
            sp.wait_ge(stored, 16 * NT)

        @block.gpsimd
        def _(pool):
            chain = [0]

            def link(ins):
                chain[0] += 1
                ins.then_inc(pool_chain, 1)
                pool.wait_ge(pool_chain, chain[0])

            nc.gpsimd.iota(iota_i[:, 0:NT * WIN], [[1, NT * WIN]], base=0, channel_multiplier=0).then_inc(consts, 1)
            nc.gpsimd.iota(win_i[:, :], [[P, ET // TPB], [WSTEP, TPB]], base=-WBACK, channel_multiplier=0).then_inc(consts, 1)
            nc.gpsimd.memset(f(ones_r[:, :]), 1.0).then_inc(consts, 1)
            link(nc.gpsimd.memset(ident[:, :], 0.0))
            nc.gpsimd.affine_select(out=ident[:, :], in_=ident[:, :], compare_op=ALU.not_equal, fill=1.0, base=0,
                                    pattern=[[-1, P]], channel_multiplier=1).then_inc(consts, 1)
            nc.gpsimd.memset(nhalf[:, :], -0.5).then_inc(consts, 1)
            pool.wait_ge(tables, 2)
            link(nc.gpsimd.iota(iota_i[:, 0:NT * GRP], [[N, NT], [1, GRP]], base=0, channel_multiplier=0))
            nc.gpsimd.tensor_copy(iotaG[:, :, :].rearrange("p h d -> p (h d)"),
                                  iota_i[:, 0:NT * GRP]).then_inc(consts, 1)

            def minus_mean(t):
                pool.wait_ge(summed, t + 1)
                nc.gpsimd.tensor_scalar(nmean[:, t:t + 1], xsum[:, t:t + 1], -1.0 / D, None, ALU.mult).then_inc(centred, 1)

            def inverse_deviation(layer, t):
                link(nc.gpsimd.tensor_tensor(rstd[:, layer, t:t + 1], var_e[:, layer, t:t + 1], nhalf[:, :], ALU.pow))

            def norm0(t):
                pool.wait_ge(squared, t + 1)
                link(nc.gpsimd.tensor_scalar(var_e[:, 0, t:t + 1], xsq[:, t:t + 1], 1.0 / D, EPS, ALU.mult, ALU.add))
                inverse_deviation(0, t)
                nc.gpsimd.tensor_tensor(nmr[:, 0, t:t + 1], nmean[:, t:t + 1], rstd[:, 0, t:t + 1], ALU.mult).then_inc(normed, 1)

            def norm1(t):
                pool.wait_ge(stats, t + 1)
                link(nc.gpsimd.tensor_scalar(var_e[:, 1, t:t + 1], mv[:, t, 1:2], EPS, None, ALU.add))
                inverse_deviation(1, t)
                nc.gpsimd.tensor_scalar(nmr[:, 1, t:t + 1], mv[:, t, 0:1], rstd[:, 1, t:t + 1], -1.0,
                                        ALU.mult, ALU.mult).then_inc(normed, 1)

            def add_bv(t):
                pool.wait_ge(relu, t + 1)
                nc.gpsimd.tensor_tensor(xs[:, t, :], xs[:, t, :], bv_sb[:, :], ALU.add).then_inc(res_ready, 1)

            pool.wait_ge(consts, 5)
            minus_mean(0)
            for t in range(NT):
                if t + 1 < NT:
                    minus_mean(t + 1)
                norm0(t)
                if t == 0:
                    pool.wait_ge(ld_bv, 16)
                if t:
                    add_bv(t - 1)
            add_bv(NT - 1)
            pool.wait_ge(ld_b, 32)
            link(nc.gpsimd.tensor_scalar(b_sb[:, :], b_sb[:, :], alpha[:, :], None, ALU.mult))

            def fill(i):
                if i >= 2:
                    pool.wait_ge(pT_ps, 2 * (i - 1))
                else:
                    link(nc.gpsimd.memset(pr[i][:, :], 0.0))
                nc.gpsimd.tensor_scalar(pr[i % 2][:, :], pr[i % 2][:, :], 0.0, negc[:, i:i + 1],
                                        ALU.mult, ALU.add).then_inc(filled, 1)

            pool.wait_ge(c_ready, 1)
            pool.wait_ge(proj, NPROJ)
            fill(0)
            fill(1)
            for i in range(1, NT + 2):
                if i + 1 < NT:
                    fill(i + 1)
                if i >= 2:
                    norm1(i - 2)
                    pool.wait_ge(relu, NT + i - 1)
                    link(nc.gpsimd.tensor_tensor(xs[:, i - 2, :], xs[:, i - 2, :], b_sb[:, :], ALU.add))
                    nc.gpsimd.tensor_tensor(xs[:, i - 2, :], xs[:, i - 2, :], h2f[i % 2][:, :],
                                            ALU.add).then_inc(res2_ready, 1)

        @block.scalar
        def _(act):
            act.dma_start(bqk[:, 0, :], bq_d).then_inc(ld_bqk, 16)
            act.dma_start(bqk[:, 1, :], bk_d).then_inc(ld_bqk, 16)
            act.dma_start(alpha[:, :], alpha_d.partition_broadcast(P)).then_inc(ld_b, 16)
            groups = [0]
            his = [0]

            def norm_relu(layer, t, out):
                act.wait_ge(normed, layer * NT + t + 1)
                nc.scalar.activation(out, xs[:, t, :], ACT.Relu, bias=nmr[:, layer, t:t + 1],
                                     scale=rstd[:, layer, t:t + 1]).then_inc(relu, 1)

            for step, n, *to in STEPS:
                if step == "splitw":
                    act.wait_ge(consts, 1)
                    nc.scalar.activation(iotaL[:, :, :], bcast(iota_i[:, 0:P], 2, BATCH), ACT.Copy).then_inc(tables, 1)
                    nc.scalar.activation(iotaW[:, :, :], bcast(iota_i[:, 0:NT * WIN], 2, BATCH), ACT.Copy,
                                         bias=1.0).then_inc(tables, 1)
                    for q in range(2):
                        ks = slice(2 * q, 2 * q + 2)
                        act.wait_ge(ld_wq[q], 16)
                        nc.scalar.activation(wq[0][:, ks, :], wq_raw[:, ks, :], ACT.Copy, scale=SCALE).then_inc(w_hi, 1)
                        act.wait_ge(ld_wk[q], 16)
                        nc.scalar.activation(wk[0][:, ks, :], wk_raw[:, ks, :], ACT.Copy).then_inc(w_hi, 1)
                    act.wait_ge(vec_ready, 1)
                    nc.scalar.activation(b_rep[0][:, :, :, :], bcast(bqk[:, :, :], 3, P), ACT.Copy).then_inc(vec_ready, 1)
                elif step == "sum":
                    if n % 2 == 0:
                        act.wait_ge(ld_x[n // 2], 16)
                    nc.scalar.activation(h1[:, n, :], xs[:, n, :], ACT.Copy, accum_out=xsum[:, n:n + 1]).then_inc(summed, 1)
                elif step == "squares":
                    act.wait_ge(centred, n + 1)
                    nc.scalar.activation(h1[:, n, :], xs[:, n, :], ACT.Square, bias=nmean[:, n:n + 1],
                                         accum_out=xsq[:, n:n + 1]).then_inc(squared, 1)
                elif step == "wv":
                    act.wait_ge(ld_wv, 16)
                    ks = slice(2 * n, 2 * n + 2)
                    nc.scalar.activation(wv[0][:, ks, :], wv_raw[:, ks, :], ACT.Copy).then_inc(w_hi, 1)
                elif step == "rows":
                    norm_relu(0, n, h1[:, n, :])
                elif step == "T":
                    act.wait_ge(hT_ps, n + 1)
                    nc.scalar.activation(hT[0][:, :, n * P:(n + 1) * P],
                                         bank[6 + n % 2][:, :].rearrange("p (k c) -> p k c", k=KD),
                                         ACT.Copy).then_inc(hT_hi, 1)
                elif step == "count":
                    for g in range(NG):
                        if n <= LAST[g] // BATCH < to[0]:
                            act.wait_ge(oh_used, LAST[g] // BATCH + 1)
                            nc.scalar.activation(A[:, :, g * GRP:(g + 1) * GRP],
                                                 bank[g % 2][:, :].rearrange("p (h d) -> p h d", h=NT),
                                                 ACT.Copy).then_inc(count_kept, 1)
                elif step in ("M", "u", "G", "V"):
                    i = proj_index((step, n))
                    ps = bank[2 + i % 4]
                    act.wait_ge(proj, i + 1)
                    if step == "M":
                        nc.scalar.activation(M[0][:, n, :], ps[:, :], ACT.Copy).then_inc(proj_hi, 1)
                    elif step == "u":
                        nc.scalar.activation(u_sb[:, :], ps[:, :], ACT.Copy).then_inc(proj_hi, 1)
                    elif step == "G":
                        half, m = n // KD, n % KD
                        if n == 0:
                            act.wait_ge(proj_lo, proj_index(("g", 0)) + 1)
                        nc.scalar.activation(GT[0][:, 4 * half:4 * half + 4, m, :],
                                             ps[:, :].rearrange("p (t c) -> p t c", t=4),
                                             ACT.Identity, bias=g0[:, m:m + 1]).then_inc(proj_hi, 1)
                    else:
                        if n == 0:
                            act.wait_ge(c_ready, 1)
                        nc.scalar.activation(V[0][:, n, :], ps[:, :], ACT.Copy).then_inc(proj_hi, 1)

            act.wait_ge(deg_ps, 1)
            for q in range(2):
                nc.scalar.activation(dcopy[0:1, q * HALF:(q + 1) * HALF], bank[6 + q][0:1, :], ACT.Copy,
                                     accum_out=dsum[0:1, q:q + 1]).then_inc(deg_sum, 1)

            for i in range(NT + 2):
                if 1 <= i <= NT:
                    j = i - 1
                    if j >= 2:
                        act.wait_ge(attended, j - 1)
                    for q in range(2):
                        act.wait_ge(pT_ps, 2 * j + q + 1)
                        nc.scalar.activation(pT[j % 2][0][:, 4 * q:4 * q + 4, :],
                                             bank[q][:, :].rearrange("p (b c) -> p b c", b=4),
                                             ACT.Copy).then_inc(pT_hi, 1)
                if i < NT:
                    act.wait_ge(maxed, i + 1)
                    nc.scalar.activation(pr[i % 2][:, :], pr[i % 2][:, :], ACT.Exp, bias=negmax[:, i:i + 1],
                                         accum_out=rowsum[:, i:i + 1]).then_inc(expd, 1)
                if i == 3:
                    act.wait_ge(ld_wt, 16)
                    nc.scalar.activation(wt[0][:, :, :], wt_raw[:, :, :], ACT.Copy).then_inc(w_hi, 1)
                if i >= 2:
                    j = i - 2
                    if j >= 2:
                        act.wait_ge(h2_lo, j - 1)
                        act.wait_ge(res2_ready, j - 1)
                    norm_relu(1, j, h2f[j % 2][:, :])
                    act.wait_ge(relu, NT + j + 1)
                    nc.scalar.activation(h2[0][:, j, :], h2f[j % 2][:, :], ACT.Copy).then_inc(h2_hi, 1)

            for n in range(2 * KD):
                half, m = n // KD, n % KD
                act.wait_ge(agg_ps, n + 1)
                nc.scalar.activation(agT[0][:, m, half * HALF:(half + 1) * HALF], bank[AGG_BANK[n]][:, :],
                                     ACT.Copy).then_inc(agg_hi, 1)

        @block.vector
        def _(dve):
            chain = [0]

            def link(ins):
                chain[0] += 1
                ins.then_inc(dve_chain, 1)
                dve.wait_ge(dve_chain, chain[0])

            dve.wait_ge(ld_edges, 32)
            nc.vector.tensor_scalar(key_i[0][:, :], src_i[:, :], P - 1, None, ALU.bitwise_and)
            nc.vector.tensor_scalar(key_i[1][:, :], src_i[:, :], N - P, None, ALU.bitwise_and)
            dve.wait_ge(consts, 2)
            link(nc.vector.tensor_scalar(win0[:, :], win_i[:, :], 0.0, float(N - WIN), ALU.max, ALU.min))
            link(nc.vector.tensor_tensor(key_t[0][:, :], dst_i[:, :], win0[:, :], ALU.subtract))
            nc.vector.tensor_copy(lo_b[:, :], key_i[0][:, :])
            nc.vector.scalar_tensor_tensor(out=key_t[1][:, :], in0=key_i[1][:, :], scalar=float(WIN) / P,
                                           in1=key_t[0][:, :], op0=ALU.mult, op1=ALU.add)
            link(nc.vector.tensor_scalar(key_t[2][:, :], key_t[0][:, :], float(WIN), None, ALU.is_lt))
            link(nc.vector.scalar_tensor_tensor(out=key_t[3][:, :], in0=key_t[0][:, :], scalar=0.0,
                                                in1=key_t[2][:, :], op0=ALU.is_ge, op1=ALU.mult))
            link(nc.vector.scalar_tensor_tensor(out=key_b[:, :], in0=key_t[1][:, :], scalar=1.0,
                                                in1=key_t[3][:, :], op0=ALU.add, op1=ALU.mult))
            dve.wait_ge(tables, 2)

            def one_hots(a, b):
                for q in range(a, b):
                    if q >= RING:
                        dve.wait_ge(oh_used, q - RING + 1)
                    tiles = slice(BATCH * q, BATCH * q + BATCH)
                    nc.vector.tensor_tensor(ohL[:, q % RING, :, :], iotaL[:, :, :], bcast(lo_b[:, tiles], 1, P), ALU.is_equal)
                    nc.vector.tensor_tensor(ohW[:, q % RING, :, :, :].rearrange("p h d b -> p (h d) b"), iotaW[:, :, :],
                                            bcast(key_b[:, tiles], 1, NT * WIN), ALU.is_equal).then_inc(oh_ready, 1)

            def row_stats(t):
                link(nc.vector.bn_stats(bn[:, t, :], xs[:, t, :]))
                nc.vector.bn_aggr(mv[:, t, :], bn[:, t, :]).then_inc(stats, 1)

            def split_lo(n, hl, raw, ks=slice(0, KD), scale=1.0):
                dve.wait_ge(w_hi, n)
                nc.vector.scalar_tensor_tensor(out=hl[1][:, ks, :], in0=raw[:, ks, :], scalar=scale, in1=f(hl[0][:, ks, :]),
                                               op0=ALU.mult, op1=ALU.subtract).then_inc(w_lo, 1)

            for step, n, *to in VSTEPS:
                if step == "splitw":
                    dve.wait_ge(ld_bqk, 32)
                    link(nc.vector.tensor_scalar(bqk[:, 0, :], bqk[:, 0, :], SCALE, None, ALU.mult))
                    nc.vector.tensor_tensor(bprod[:, :], bqk[:, 0, :], bqk[:, 1, :], ALU.mult).then_inc(vec_ready, 1)
                    one_hots(0, START)
                    for q in range(2):
                        split_lo(2 * q + 1, wq, wq_raw, slice(2 * q, 2 * q + 2), SCALE)
                        split_lo(2 * q + 2, wk, wk_raw, slice(2 * q, 2 * q + 2))
                    dve.wait_ge(vec_ready, 2)
                    nc.vector.tensor_tensor(b_rep[1][:, :, :, :], bcast(bqk[:, :, :], 3, P), f(b_rep[0][:, :, :, :]),
                                            ALU.subtract).then_inc(vec_ready, 1)
                elif step == "count":
                    one_hots(max(n, START), to[0])
                elif step == "wv":
                    dve.wait_ge(ld_wv, 16)
                    split_lo(5 + n, wv, wv_raw, slice(2 * n, 2 * n + 2))
                elif step in ("sum", "squares", "rows", "Ma"):
                    pass
                elif step == "T":
                    dve.wait_ge(hT_hi, n + 1)
                    hi = hT[0][:, :, n * P:(n + 1) * P]
                    nc.vector.tensor_tensor(hT[1][:, :, n * P:(n + 1) * P],
                                            bank[6 + n % 2][:, :].rearrange("p (k c) -> p k c", k=KD), f(hi),
                                            ALU.subtract).then_inc(hT_lo, 1)
                elif step == "g":
                    i = proj_index((step, n))
                    dve.wait_ge(proj, i + 1)
                    dve.wait_ge(consts, 6)
                    for m in range(KD):
                        ins = nc.vector.tensor_tensor_reduce(
                            out=diag_g[:, :], in0=bank[2 + i % 4][:, m * P:(m + 1) * P], in1=ident[:, :], scale=1.0,
                            scalar=0.0, op0=ALU.mult, op1=ALU.add, accum_out=g0[:, m:m + 1])
                        if m < KD - 1:
                            link(ins)
                    ins.then_inc(proj_lo, 1)
                elif step == "u":
                    i = proj_index((step, n))
                    dve.wait_ge(proj_hi, hi_before(i + 1))
                    nc.vector.memset(dbad[:, :], 0.0).then_inc(proj_lo, 1)
                elif step == "c":
                    dve.wait_ge(relu, n + 1)
                    dve.wait_ge(proj_hi, hi_before(proj_index(("u", 0)) + 1))
                    link(nc.vector.tensor_tensor_reduce(out=uh[:, :], in0=h1[:, n, :], in1=u_sb[:, :], scale=1.0,
                                                        scalar=0.0, op0=ALU.mult, op1=ALU.add, accum_out=c_f[:, n:n + 1]))
                    if n == NT - 1:
                        dve.wait_ge(bb_kept, 1)
                        link(nc.vector.tensor_scalar(negc[:, :], c_f[:, :], bb[:, :], None, ALU.add))
                        nc.vector.tensor_scalar(negc[:, :], negc[:, :], -1.0, NEG, ALU.mult, ALU.add).then_inc(c_ready, 1)
                else:
                    i = proj_index((step, n))
                    ps = bank[2 + i % 4]
                    dve.wait_ge(proj_hi, hi_before(i + 1))
                    if (step, n) == ("M", 0):
                        dve.wait_ge(bb_ps, 1)
                        nc.vector.tensor_reduce(bb[:, :], bank[7][:, 0:KD], AX.X, ALU.add).then_inc(bb_kept, 1)
                    if step == "M":
                        ins = nc.vector.tensor_tensor(M[1][:, n, :], ps[:, :], f(M[0][:, n, :]), ALU.subtract)
                    elif step == "G":
                        half, m = n // KD, n % KD
                        ins = nc.vector.scalar_tensor_tensor(
                            out=GT[1][:, 4 * half:4 * half + 4, m, :], in0=ps[:, :].rearrange("p (t c) -> p t c", t=4),
                            scalar=g0[:, m:m + 1], in1=f(GT[0][:, 4 * half:4 * half + 4, m, :]),
                            op0=ALU.add, op1=ALU.subtract)
                    else:
                        ins = nc.vector.tensor_tensor(V[1][:, n, :], ps[:, :], f(V[0][:, n, :]), ALU.subtract)
                    ins.then_inc(proj_lo, 1)

            dve.wait_ge(deg_ps, 1)
            for q in range(2):
                dve.wait_ge(deg_sum, q + 1)
                last = nc.vector.tensor_reduce(dmax[0:1, q:q + 1], bank[6 + q][0:1, :], AX.X, ALU.max)
            link(last)
            nc.vector.tensor_scalar(dbad[0:1, 0:1], dsum[0:1, 0:1], dsum[0:1, 1:2], float(E), ALU.add, ALU.not_equal)
            link(nc.vector.tensor_scalar(dbad[0:1, 1:2], dmax[0:1, 0:1], dmax[0:1, 1:2], float(EXACT), ALU.max, ALU.is_ge))
            nc.vector.tensor_tensor(flag[0:1, :], dbad[0:1, 0:1], dbad[0:1, 1:2], ALU.add).then_inc(flag_ready, 1)
            dve.wait_ge(flag_ready, 1)
            general = nc.vector.value_load(flag[0:1, 0:1], min_val=0, max_val=2)
            with dve.If(general > 0):
                dve.wait_ge(res_ready, NT)
                nc.vector.tensor_scalar(gen_key[:, :].bitcast(I32), src_i[:, :], P - 1, None, ALU.bitwise_and).then_inc(gen_prep, 1)
                dve.wait_ge(gen_prep, 1)
                nc.vector.tensor_copy(gen_lo[:, :], gen_key[:, :].bitcast(I32)).then_inc(gen_prep, 1)
                dve.wait_ge(gen_prep, 2)
                nc.vector.memset(gen0[:, :], 0.0)
                nc.vector.tensor_scalar(gen_i[:, :], src_i[:, :], N - P, None, ALU.bitwise_and).then_inc(gen_prep, 1)
                dve.wait_ge(gen_prep, 3)
                nc.vector.scalar_tensor_tensor(out=gen_key[:, :], in0=gen_i[:, :], scalar=float(N) / P, in1=dst_i[:, :],
                                               op0=ALU.mult, op1=ALU.add).then_inc(gen_prep, 1)
                nc.vector.memset(dbad[:, :], 0.0).then_inc(gen_R_s, 1)
                dve.wait_ge(gen_prep, 4)
                dve.wait_ge(consts, 6)
                with dve.Fori(0, NG) as g:
                    with dve.Fori(0, (ET // 2)) as q:
                        dve.wait_ge(gen_used, g * (ET // 2) + q + 1)
                        for u in range(2):
                            nc.vector.tensor_scalar(genL[:, u, :], iotaL[:, :, 0], gen_lo[:, bass.ds(2 * q + u, 1)], None,
                                                    ALU.is_equal)
                            last = nc.vector.tensor_scalar(genW[:, u, :], iotaG[:, :, :].rearrange("p h d -> p (h d)"),
                                                           gen_key[:, bass.ds(2 * q + u, 1)], None, ALU.is_equal)
                        last.then_inc(gen_ready, 1)
                    nc.vector.tensor_scalar(iotaG[:, :, :], iotaG[:, :, :], float(GRP), None, ALU.add).then_inc(gen_iota, 1)
                    dve.wait_ge(gen_ps, g + 1)
                    got = bank[0][:, :].rearrange("p (h d) -> p h d", h=NT)
                    nc.vector.tensor_copy(A[:, :, bass.ds(g * GRP, GRP)], got).then_inc(gen_A, 1)
                    dve.wait_ge(gen_A, g + 1)
                    nc.vector.tensor_tensor(R[:, :, bass.ds(g * GRP, GRP)], got, A_f[:, :, bass.ds(g * GRP, GRP)],
                                            ALU.subtract).then_inc(gen_R_s, 1)
                    dve.wait_ge(gen_iota, g + 1)
                    dve.wait_ge(gen_R_s, g + 2)
                for h in range(NT):
                    if h:
                        dve.wait_ge(gen_deg, h)
                    nc.vector.tensor_copy(gen_R[:, :], R[:, h, :]).then_inc(gen_stage, 1)
                dve.wait_ge(gen_deg, NT)
            nc.vector.memset(dbad[:, :], 0.0).then_inc(counts_final, 1)

            def degree_columns():
                for j in range(NT):
                    ins = nc.vector.tensor_tensor_reduce(
                        out=diag_d[:, :], in0=bank[6 + j // 4][:, j % 4 * P:(j % 4 + 1) * P], in1=ident[:, :], scale=1.0,
                        scalar=0.0, op0=ALU.mult, op1=ALU.add, accum_out=deg[:, j:j + 1])
                    if j < NT - 1:
                        link(ins)
                ins.then_inc(deg_kept, 1)
                dve.wait_ge(deg_kept, 1)
                link(nc.vector.tensor_scalar(deg[:, :], deg[:, :], 1.0, None, ALU.max))
                link(nc.vector.reciprocal(rdeg[:, :], deg[:, :]))
                dve.wait_ge(ld_b, 32)
                nc.vector.tensor_scalar(rdeg[:, :], rdeg[:, :], alpha[:, :], None, ALU.mult).then_inc(rdeg_ready, 1)

            def h2_lo_part(j):
                dve.wait_ge(h2_hi, j + 1)
                nc.vector.tensor_tensor(h2[1][:, j, :], h2f[j % 2][:, :], f(h2[0][:, j, :]), ALU.subtract).then_inc(h2_lo, 1)

            for i in range(NT + 2):
                if i < NT:
                    dve.wait_ge(filled, i + 1)
                    for q in range(2):
                        dve.wait_ge(scored, 2 * i + q + 1)
                        cols = slice(q * HALF, (q + 1) * HALF)
                        ins = nc.vector.copy_predicated(pr[i % 2][:, cols], A_i[:, i, cols], bank[2 + (2 * i + q) % 4][:, :])
                        ins.then_inc(masked, 1)
                    dve.wait_ge(masked, 2 * i + 2)
                    nc.vector.tensor_reduce(negmax[:, i:i + 1], pr[i % 2][:, :], AX.X, ALU.max, negate=True).then_inc(maxed, 1)
                if i == 0:
                    degree_columns()
                if i == 3:
                    dve.wait_ge(ld_wt, 16)
                    split_lo(7, wt, wt_raw)
                if 1 <= i <= NT:
                    j = i - 1
                    for q in range(2):
                        dve.wait_ge(pT_hi, 2 * j + q + 1)
                        nc.vector.tensor_tensor(pT[j % 2][1][:, 4 * q:4 * q + 4, :],
                                                bank[q][:, :].rearrange("p (b c) -> p b c", b=4),
                                                f(pT[j % 2][0][:, 4 * q:4 * q + 4, :]), ALU.subtract).then_inc(pT_lo, 1)
                if i >= 3:
                    h2_lo_part(i - 3)
                if i >= 2:
                    j = i - 2
                    dve.wait_ge(expd, j + 1)
                    link(nc.vector.reciprocal(rinv[:, j:j + 1], rowsum[:, j:j + 1]))
                    dve.wait_ge(attended, j + 1)
                    nc.vector.scalar_tensor_tensor(out=xs[:, j, :], in0=bank[6 + j % 2][:, :], scalar=rinv[:, j:j + 1],
                                                   in1=xs[:, j, :], op0=ALU.mult, op1=ALU.add).then_inc(x2_ready, 1)
                    dve.wait_ge(x2_ready, j + 1)
                    row_stats(j)
            h2_lo_part(NT - 1)

            with dve.If(general > 0):
                for k in range(2 * NT):
                    half, h = k // NT, k % NT
                    if k == 0:
                        dve.wait_ge(h2_lo, NT)
                        dve.wait_ge(res2_ready, NT)
                    if k >= 2:
                        dve.wait_ge(agg_used, k - 1)
                    nc.vector.tensor_copy(r_st[k % 2][:, :], R[:, h, half * HALF:(half + 1) * HALF]).then_inc(agg_stage, 1)

            for n in range(2 * KD):
                half, m = n // KD, n % KD
                cols = slice(half * HALF, (half + 1) * HALF)
                dve.wait_ge(agg_hi, n + 1)
                nc.vector.tensor_tensor(agT[1][:, m, cols], bank[AGG_BANK[n]][:, :], f(agT[0][:, m, cols]),
                                        ALU.subtract).then_inc(agg_lo, 1)
            dve.wait_ge(rdeg_ready, 1)
            for j in range(NT):
                dve.wait_ge(res2_ready, j + 1)
                dve.wait_ge(out_ps, j + 1)
                nc.vector.scalar_tensor_tensor(out=o_sb[:, j, :], in0=bank[2 + j % 4][:, :], scalar=rdeg[:, j:j + 1],
                                               in1=xs[:, j, :], op0=ALU.mult, op1=ALU.add).then_inc(out_ready, 1)

        @block.tensor
        def _(pe):
            mm = nc.tensor.matmul

            def product(out, lhs, rhs, pairs, first, final):
                for k, (a, b) in enumerate(pairs):
                    mm(out, lhs[0][a], rhs[0][b], start=(first and k == 0), stop=False)
                    mm(out, lhs[0][a], rhs[1][b], start=False, stop=False)
                    last = mm(out, lhs[1][a], rhs[0][b], start=False, stop=(final and k == len(pairs) - 1))
                return last

            def three_pass(out, lhs, rhs, pairs):
                return product(out, lhs, rhs, pairs, True, True)

            def count(a, b):
                for q in range(a, b):
                    pe.wait_ge(oh_ready, q + 1)
                    for u in range(BATCH):
                        t = BATCH * q + u
                        w = window(t)
                        for g, c0, c1 in pieces(t):
                            if FIRST[g] == t and g >= 2:
                                pe.wait_ge(count_kept, g - 1)
                            out = bank[g % 2][:, :].rearrange("p (h d) -> p h d", h=NT)[:, :, c0 - g * GRP:c1 - g * GRP]
                            last = mm(out, ohL[:, q % RING, :, u], ohW[:, q % RING, :, c0 - w:c1 - w, u],
                                      start=(FIRST[g] == t), stop=(LAST[g] == t), skip_group_check=True)
                    last.then_inc(oh_used, 1)

            every = slice(None)

            def cols(k, m, width=P):
                return (every, k, slice(m * width, (m + 1) * width))

            for step, n, *to in STEPS:
                if step == "count":
                    count(n, to[0])
                elif step == "T":
                    pe.wait_ge(relu, n + 1)
                    if n == 1:
                        pe.wait_ge(bb_kept, 1)
                    if n >= 2:
                        pe.wait_ge(hT_lo, n - 1)
                    for k in range(KD):
                        last = nc.tensor.transpose(bank[6 + n % 2][:, k * P:(k + 1) * P], h1[:, n, k * P:(k + 1) * P],
                                                   ident[:, :])
                    last.then_inc(hT_ps, 1)
                elif step == "Ma":
                    pe.wait_ge(w_lo, 2)
                    for m in range(KD):
                        product(bank[2 + m][:, :], wq, wk, [(cols(k, m), cols(k, 0, D)) for k in (0, 1)], True, False)
                    pe.wait_ge(vec_ready, 1)
                    pe.wait_ge(consts, 4)
                    mm(bank[7][:, 0:KD], f(ones_r[:, :]), bprod[:, :], start=True, stop=True).then_inc(bb_ps, 1)
                elif step in ("M", "u", "g", "G", "V"):
                    i = proj_index((step, n))
                    ps = bank[2 + i % 4]
                    if i >= 4:
                        pe.wait_ge(proj_lo, i - 3)
                    if step == "M":
                        pe.wait_ge(w_lo, 4)
                        last = product(ps[:, :], wq, wk, [(cols(k, n), cols(k, 0, D)) for k in (2, 3)], False, True)
                    elif step == "u":
                        pe.wait_ge(vec_ready, 3)
                        last = three_pass(ps[:, :], b_rep, wq, [((every, 1, k, every), cols(k, 0, D)) for k in range(KD)])
                    elif step == "g":
                        last = three_pass(ps[:, :], b_rep, wk, [((every, 0, k, every), cols(k, 0, D)) for k in range(KD)])
                    elif step == "G":
                        half, m = n // KD, n % KD
                        if m == 0:
                            pe.wait_ge(hT_lo, 4 * (half + 1))
                            pe.wait_ge(proj_lo, KD)
                        last = three_pass(ps[:, :], M, hT, [(cols(k, m), cols(k, half, HALF)) for k in range(KD)])
                    else:
                        if n == 0:
                            pe.wait_ge(w_lo, 6)
                        last = three_pass(ps[:, :], hT, wv, [(cols(k, n), cols(k, 0, D)) for k in range(KD)])
                    last.then_inc(proj, 1)

            def scores(i):
                for q in range(2):
                    if i < 2:
                        pe.wait_ge(proj_lo, NPROJ)
                    else:
                        pe.wait_ge(masked, 2 * (i - 2) + q + 1)
                    three_pass(bank[2 + (2 * i + q) % 4][:, :], GT, hT,
                               [((every, i, k, every), cols(k, q, HALF)) for k in range(KD)]).then_inc(scored, 1)

            def degrees(rows, first, stop):
                for n, row in enumerate(rows):
                    for q in range(2):
                        last = mm(bank[6 + q][:, :], ones_r[:, :], row[:, q * HALF:(q + 1) * HALF],
                                  start=(first and n == 0), stop=stop and n == len(rows) - 1, skip_group_check=True)
                return last

            pe.wait_ge(count_kept, NG)
            pe.wait_ge(hT_lo, NT)
            degrees([A[:, h, :] for h in range(NT)], True, True).then_inc(deg_ps, 1)
            scores(0)
            scores(1)
            pe.wait_ge(flag_ready, 1)
            general = nc.tensor.value_load(flag[0:1, 0:1], min_val=0, max_val=2)
            with pe.If(general > 0):
                pe.wait_ge(gen_prep, 4)
                mm(bank[0][:, 0:P], gen0[:, 0:P], gen0[:, 0:P], start=True, stop=True).then_inc(gen_used, 1)
                with pe.Fori(0, NG) as g:
                    pe.wait_ge(gen_R_s, g + 1)
                    mm(bank[0][:, :], gen0[:, 0:P], gen0[:, :], start=True, stop=False, skip_group_check=True)
                    with pe.Fori(0, (ET // 2)) as q:
                        pe.wait_ge(gen_ready, g * (ET // 2) + q + 1)
                        for u in range(2):
                            last = mm(bank[0][:, :], genL[:, u, :], genW[:, u, :], start=False, stop=False,
                                      skip_group_check=True)
                        last.then_inc(gen_used, 1)
                    mm(bank[0][:, :], gen0[:, 0:P], gen0[:, :], start=False, stop=True,
                       skip_group_check=True).then_inc(gen_ps, 1)
                pe.wait_ge(gen_R_s, NG + 1)
                degrees([A[:, h, :] for h in range(NT)], True, False)
                for h in range(NT):
                    pe.wait_ge(gen_stage, h + 1)
                    degrees([gen_R[:, :]], False, h == NT - 1).then_inc(gen_deg, 1)

            for i in range(NT + 2):
                if 2 <= i < NT:
                    scores(i)
                if 1 <= i <= NT:
                    j = i - 1
                    pe.wait_ge(expd, j + 1)
                    if j == 0:
                        pe.wait_ge(counts_final, 1)
                    for q in range(2):
                        if j >= 1:
                            pe.wait_ge(pT_lo, 2 * (j - 1) + q + 1)
                        for b in range(4):
                            c = (4 * q + b) * P
                            last = nc.tensor.transpose(bank[q][:, b * P:(b + 1) * P], pr[j % 2][:, c:c + P], ident[:, :])
                        last.then_inc(pT_ps, 1)
                if i >= 2:
                    j = i - 2
                    pe.wait_ge(pT_lo, 2 * (j + 1))
                    if j == 0:
                        pe.wait_ge(deg_kept, 1)
                    if j >= 2:
                        pe.wait_ge(x2_ready, j - 1)
                    if i == NT + 1:
                        aggregate(nc, pe, mm, bank, h2, A, range(0, NT - 2), range(0, KD), masked, h2_lo)
                    three_pass(bank[6 + j % 2][:, :], pT[j % 2], V,
                               [((every, b, every), (every, b, every)) for b in range(NT)]).then_inc(attended, 1)

            pe.wait_ge(h2_lo, NT - 1)
            aggregate(nc, pe, mm, bank, h2, A, range(NT - 2, NT - 1), range(0, KD), None, None)
            pe.wait_ge(pT_lo, 2 * NT)
            pe.wait_ge(x2_ready, NT)
            aggregate(nc, pe, mm, bank, h2, A, range(0, NT - 1), range(KD, 2 * KD), None, None)
            pe.wait_ge(h2_lo, NT)
            with pe.If(general > 0):
                for k in range(2 * NT):
                    half, h = k // NT, k % NT
                    pe.wait_ge(agg_stage, k + 1)
                    for m in range(KD):
                        for hl in range(2):
                            last = mm(bank[AGG_BANK[half * KD + m]][:, :], h2[hl][:, h, m * P:(m + 1) * P],
                                      r_st[k % 2][:, :], start=False, stop=False, skip_group_check=True)
                    last.then_inc(agg_used, 1)
            for n in range(2 * KD):
                half, m = n // KD, n % KD
                for hl in range(2):
                    last = mm(bank[AGG_BANK[n]][:, :], h2[hl][:, NT - 1, m * P:(m + 1) * P],
                              A[:, NT - 1, half * HALF:(half + 1) * HALF], start=False, stop=(hl == 1),
                              skip_group_check=True)
                last.then_inc(agg_ps, 1)

            pe.wait_ge(w_lo, 7)
            for j in range(NT):
                if j % 4 == 0:
                    pe.wait_ge(agg_lo, KD * (j // 4 + 1))
                if j >= 4:
                    pe.wait_ge(out_ready, j - 3)
                three_pass(bank[2 + j % 4][:, :], agT, wt,
                           [(cols(k, j), cols(k, 0, D)) for k in range(KD)]).then_inc(out_ps, 1)


AGG_BANK = [2, 3, 4, 5, 0, 1, 6, 7]


def aggregate(nc, pe, mm, bank, h2, A, rows, groups, masked, h2_lo):
    for h in rows:
        if masked is not None:
            if h == 0:
                pe.wait_ge(masked, 2 * NT)
            pe.wait_ge(h2_lo, h + 1)
        for n in groups:
            half, m = n // KD, n % KD
            for hl in range(2):
                mm(bank[AGG_BANK[n]][:, :], h2[hl][:, h, m * P:(m + 1) * P], A[:, h, half * HALF:(half + 1) * HALF],
                   start=(h == 0 and hl == 0), stop=False, skip_group_check=True)


def kernel(**inputs):
    import numpy as _np
    import concourse.bacc as _bacc
    from concourse import mybir as _mybir
    from concourse.bass_utils import run_bass_kernel_spmd as _run

    def columns(v):
        return _np.asarray(v).reshape(-1, P).T

    layout = {
        "x": _np.asarray(inputs["x"]),
        "src": columns(inputs["src"]), "dst": columns(inputs["dst"]),
        "wqT": _np.asarray(inputs["L0_gnn_Wq"]).T, "wkT": _np.asarray(inputs["L0_gnn_Wk"]).T,
        "wv": _np.asarray(inputs["L0_gnn_Wv"]), "wT": _np.asarray(inputs["L1_gnn_W"]).T,
        "bq": columns(inputs["L0_gnn_bq"]), "bk": columns(inputs["L0_gnn_bk"]),
        "bv": _np.asarray(inputs["L0_gnn_bv"]), "b": _np.asarray(inputs["L1_gnn_b"]),
        "alpha": _np.asarray(inputs["L1_gnn_alpha"]).reshape(1),
    }
    nc = _bacc.Bacc("TRN2", target_bir_lowering=False, num_devices=1)
    arrays, args = {}, []
    for name, a in layout.items():
        a = _np.ascontiguousarray(a)
        arrays[f"in_{name}"] = a
        args.append(nc.dram_tensor(f"in_{name}", a.shape, _mybir.dt.from_np(a.dtype), kind="ExternalInput").ap())
    out = nc.dram_tensor("out_dram", (N, D), _mybir.dt.float32, kind="ExternalOutput").ap()
    gnn_kernel(nc, *args, out)
    r = _run(nc, [arrays], core_ids=[0])
    return r.results[0]["out_dram"]
```

```python
import concourse.bass as bass
from concourse import mybir
from contextlib import ExitStack

F32 = mybir.dt.float32
F32R = mybir.dt.float32r
BF16 = mybir.dt.bfloat16
I32 = mybir.dt.int32
I8 = mybir.dt.int8
ALU = mybir.AluOpType
ACT = mybir.ActivationFunctionType
AX = mybir.AxisListType

P = 128
N, D, E = 1024, 512, 33792
NT = N // P
KD = D // P
ET = E // P
HALF = N // 2
NEG = -1.0e6
EPS = 1e-5
SCALE = 1.0 / float(D) ** 0.5

WIN = 24
GRP = 64
NG = N // GRP
TPB = 33
WSTEP, WBACK = 4, 10
EXACT = 4096

BATCH = 4
NB = ET // BATCH
RING = 4


def window(t):
    return min(max(P * (t // TPB) + WSTEP * (t % TPB) - WBACK, 0), N - WIN)


def pieces(t):
    w = window(t)
    return [(g, max(w, GRP * g), min(w + WIN, GRP * g + GRP)) for g in range(w // GRP, (w + WIN - 1) // GRP + 1)]


FIRST = {g: min(t for t in range(ET) if any(p[0] == g for p in pieces(t))) for g in range(NG)}
LAST = {g: max(t for t in range(ET) if any(p[0] == g for p in pieces(t))) for g in range(NG)}


PLAN = [(("Ma", 0), ["gterms 0", "stats 0", "stats 1"], [], 0),
        (("Ma", 1), ["stats 2", "stats 3", "rows 0"], [], 2),
        (("M", 0), ["rows 1", "gsum 0"], [0], 1),
        (("M", 1), ["rows 2"], [1], 1),
        (("M", 2), ["rows 3"], [2], 1),
        (("M", 3), ["sum 4"], [3], 1),
        (("g", 0), [], [], 2),
        (("G", 0), ["sum 5", "squares 4", "sum 6"], [], 4),
        (("G", 1), ["squares 5", "rows 4", "sum 7"], [4], 4),
        (("G", 2), ["squares 6", "rows 5", "squares 7", "rows 6"], [5, 6], 3),
        (("G", 3), ["rows 7", "usum 0"], [7], 4),
        (("G", 4), ["wv 0"], [], 4),
        (("u", 0), [], [], 1),
        (("G", 5), ["wv 1", "c 0"], [], 3),
        (("G", 6), ["c 1", "csum 0", "c 2"], [], 4),
        (("G", 7), ["c 3", "csum 1", "csum 2"], [], 4),
        (("V", 0), ["c 4", "csum 3"], [], 4),
        (("V", 1), ["c 5", "csum 4"], [], 4),
        (("V", 2), ["c 6", "csum 5"], [], 4),
        (("V", 3), ["c 7", "csum 6"], [], 4),
        (("V", 4), ["csum 7"], [], 4),
        (("V", 5), [], [], 4),
        (("V", 6), [], [], NB),
        (("V", 7), [], [], 0)]
STATS0 = sum(s.startswith("stats") for _, others, _, _ in PLAN for s in others)
LATE = 3
WARM = 36
START = 1


def schedule():
    groups, at, tiles, degrees = [[("weights", 0)]], 0, 0, 0
    for step, others, transposed, batches in PLAN:
        group = [(what, int(n)) for what, n in (s.split() for s in others)]
        group.append(step)
        group += [("T", t) for t in transposed]
        tiles += len(transposed)
        if at < min(at + batches, NB):
            group.append(("count", at, min(at + batches, NB)))
            at = group[-1][2]
        if degrees < 2 and tiles == NT and at > LAST[NG // 2 * (degrees + 1) - 1] // BATCH + LATE:
            group.append(("deg", degrees))
            degrees += 1
        groups.append(group)
    assert at == NB and tiles == NT
    groups.append([("deg", q) for q in range(degrees, 2)])
    return groups


GROUPS = schedule()
STEPS = [s for group in GROUPS for s in group]
VSTEPS = [s for group in GROUPS[:1] for s in group]
VSTEPS += [s for group in GROUPS[1:] for s in sorted(group, key=lambda s: s[0] != "count")]


def kept(a, b):
    return [g for g in range(NG) if a <= LAST[g] // BATCH < b]


PROJ = [s for s in STEPS if s[0] in ("M", "u", "g", "G", "V")]
NPROJ = len(PROJ)


def hi_before(n):
    return sum(s[0] in ("M", "u", "G", "V") for s in PROJ[:n])


def gnn_kernel(nc, x_d, src_d, dst_d, wqT_d, wkT_d, wv_d, wT_d, bq_d, bk_d, bv_d, b_d, alpha_d, out_d):
    with ExitStack() as ctx:
        ctx.enter_context(nc.sbuf_tensor("arena", [P, 53150], F32))
        top = nc.sbuf_base
        start = top - 53150 * 4
        at = [start + (-start) % 32]

        def region(nbytes):
            a = at[0]
            at[0] += (nbytes + 31) // 32 * 32
            assert at[0] <= top, (at[0], top)
            return a

        def place(name, shape, dt, offset):
            return nc.alloc_sbuf_tensor_at(name, shape, dt, offset=offset)

        def small(name, shape, dt):
            size = 2 if dt == BF16 else 4
            for s in shape[1:]:
                size *= s
            return place(name, shape, dt, region(size))

        KB = 1024
        r_hT, r_G, r_V, r_A = (region(32 * KB) for _ in range(4))
        r_x, r_W0, r_W2, r_W1, r_R = region(16 * KB), region(16 * KB), region(16 * KB), region(16 * KB), region(8 * KB)

        hT = [place("hT_hi", [P, KD, N], F32R, r_hT), place("hT_lo", [P, KD, N], F32R, r_hT + 16 * KB)]
        agT = [place("agT_hi", [P, KD, N], F32R, r_hT), place("agT_lo", [P, KD, N], F32R, r_hT + 16 * KB)]
        GT = [place("GT_hi", [P, NT, KD, P], F32R, r_G), place("GT_lo", [P, NT, KD, P], F32R, r_G + 16 * KB)]
        h2 = [place("h2_hi", [P, NT, D], F32R, r_G), place("h2_lo", [P, NT, D], F32R, r_G + 16 * KB)]
        wq_raw = place("wq_raw", [P, KD, D], F32, r_G + 24 * KB)
        wk_raw = place("wk_raw", [P, KD, D], F32, r_G + 8 * KB)
        g_terms = place("g_terms", [P, KD, D], F32, r_G + 16 * KB)
        u_terms = place("u_terms", [P, KD, D], F32, r_V + 24 * KB)
        t_g = g_terms[:, 0, :]
        V = [place("V_hi", [P, NT, D], F32R, r_V), place("V_lo", [P, NT, D], F32R, r_V + 16 * KB)]
        h1 = place("h1", [P, NT, D], F32, r_V)
        wk = [place("wk_hi", [P, KD, D], F32R, r_V + 16 * KB), place("wk_lo", [P, KD, D], F32R, r_V + 24 * KB)]
        o_sb = place("o_sb", [P, NT, D], F32, r_V)
        A = place("A", [P, NT, N], F32R, r_A)
        A_f = A[:, :, :].bitcast(F32)
        A_i = A[:, :, :].bitcast(I32)
        R = place("R", [P, NT, N], I8, r_R)
        bv_sb, u_sb, uh0, t_u = (place(n, [P, D], F32, r_R + 2 * KB * i) for i, n in enumerate(("bv_sb", "u_sb", "uh0", "t_u")))
        uh = [uh0, t_u]
        xs = place("xs", [P, NT, D], F32, r_x)
        wq = [place("wq_hi", [P, KD, D], F32R, r_W0), place("wq_lo", [P, KD, D], F32R, r_W0 + 8 * KB)]
        wv = [place("wv_hi", [P, KD, D], F32R, r_W0), place("wv_lo", [P, KD, D], F32R, r_W0 + 8 * KB)]
        wv_raw = place("wv_raw", [P, KD, D], F32, r_W0 + 8 * KB)
        KEY = 1280
        iota_i = place("iota_i", [P, NT * WIN], I32, r_W2)
        win_i = place("win_i", [P, ET], I32, r_W2 + KEY)
        win0 = place("win0", [P, ET], F32, r_W2 + 2 * KEY)
        key_t = [place(f"key_t{i}", [P, ET], F32, r_W2 + (3 + i) * KEY) for i in range(4)]
        key_i = [place(f"key_i{i}", [P, ET], I32, r_W2 + (7 + i) * KEY) for i in range(2)]
        M = [place("M_hi", [P, KD, D], F32R, r_W2), place("M_lo", [P, KD, D], F32R, r_W2 + 8 * KB)]
        pr = [place(f"pr{i}", [P, N], F32, r_W0 + 4 * KB * i) for i in range(2)]
        pT = [[place(f"pT_hi{i}", [P, NT, P], F32R, r_W0 + (8 + 8 * i) * KB),
               place(f"pT_lo{i}", [P, NT, P], F32R, r_W0 + (12 + 8 * i) * KB)] for i in range(2)]
        h2f = [place(f"h2f{i}", [P, D], F32, r_W0 + (24 + 2 * i) * KB) for i in range(2)]
        r_st = [place(f"r_st{i}", [P, HALF], F32R, r_W0 + (24 + 2 * i) * KB) for i in range(2)]
        b_sb = place("b_sb", [P, D], F32, r_W0 + 28 * KB)
        diag_d = place("diag_d", [P, P], BF16, r_W0 + 30 * KB)
        ohL = place("ohL", [P, RING, P, BATCH], BF16, r_W1)
        ohW = place("ohW", [P, RING, NT, WIN, BATCH], BF16, r_W1 + RING * BATCH * P * 2)
        iotaG = place("iotaG", [P, NT, GRP], F32, r_W1 + 13 * KB)
        iotaL = place("iotaL", [P, P, BATCH], BF16, r_W1 + 15 * KB)
        dpart = place("dpart", [P, HALF], F32R, r_W1 + 10 * KB)
        dfold = place("dfold", [P, NT // 2, GRP], F32, r_W1 + 12 * KB)
        genL = place("genL", [P, 2, P], BF16, r_W1)
        genW = place("genW", [P, 2, NT * GRP], BF16, r_W1 + 1 * KB)
        gen0 = place("gen0", [P, NT * GRP], BF16, r_W1 + 3 * KB)
        gen_key = place("gen_key", [P, ET], F32, r_W1 + 4 * KB)
        gen_i = place("gen_i", [P, ET], I32, r_W1 + 6 * KB)
        gen_lo = place("gen_lo", [P, ET], F32, r_W1 + 8 * KB)
        gen_R = place("gen_R", [P, N], F32R, r_W1 + 6 * KB)
        wt = [place("wt_hi", [P, KD, D], F32R, r_W1), place("wt_lo", [P, KD, D], F32R, r_W1 + 8 * KB)]
        wt_raw = place("wt_raw", [P, KD, D], F32, r_W1 + 8 * KB)

        src_i, dst_i = small("src_i", [P, ET], I32), small("dst_i", [P, ET], I32)
        lo_b, key_b = small("lo_b", [P, ET], BF16), small("key_b", [P, ET], BF16)
        iotaW = small("iotaW", [P, NT * WIN, BATCH], BF16)
        ident, ones_r = small("ident", [P, P], F32), small("ones_r", [P, P], F32R)
        bqk = small("bqk", [P, 2, KD], F32)
        bqk_s = small("bqk_s", [P, 2, KD], F32)
        bprod, g0 = small("bprod", [P, KD], F32), small("g0", [P, KD], F32)
        bb, c_f, negc = small("bb", [P, 1], F32), small("c_f", [P, NT], F32), small("negc", [P, NT], F32)
        bn = small("bn", [P, NT, 6], F32)
        mv = small("mv", [P, NT, 2], F32)
        xsum, xsq, nmean = (small(n, [P, NT], F32) for n in ("xsum", "xsq", "nmean"))
        nhalf = small("nhalf", [P, 1], F32)
        var_e, rstd, nmr = (small(n, [P, 2, NT], F32) for n in ("var_e", "rstd", "nmr"))
        negmax, rowsum, rinv = (small(n, [P, NT], F32) for n in ("negmax", "rowsum", "rinv"))
        deg, rdeg = small("deg", [P, NT], F32), small("rdeg", [P, NT], F32)
        alpha = small("alpha", [P, 1], F32)
        dsum, dmax, dbad = small("dsum", [P, 2], F32), small("dmax", [P, 2], F32), small("dbad", [P, 2], F32)
        flag = small("flag", [P, 1], I32)

        bank = [ctx.enter_context(nc.psum_tensor(f"bank{i}", [P, 512], F32)) for i in range(8)]

        def sem(name):
            return ctx.enter_context(nc.semaphore(name))

        ld_edges, ld_wv, ld_wt = (sem(n) for n in ("ld_edges", "ld_wv", "ld_wt"))
        ld_wq, ld_wk = ([sem(f"{n}{q}") for q in range(2)] for n in ("ld_wq", "ld_wk"))
        ld_x = [sem(f"ld_x{i}") for i in range(4)]
        ld_bqk, ld_bv, ld_b, stored = sem("ld_bqk"), sem("ld_bv"), sem("ld_b"), sem("stored")
        consts = sem("consts")
        tables = sem("tables")
        pool_chain, dve_chain = sem("pool_chain"), sem("dve_chain")
        oh_ready, oh_used = sem("oh_ready"), sem("oh_used")
        count_kept = sem("count_kept")
        w_hi = sem("w_hi")
        w_lo = sem("w_lo")
        wk_lo, wv_lo = sem("wk_lo"), sem("wv_lo")
        vec_ready = sem("vec_ready")
        uh_ready, dots = sem("uh_ready"), sem("dots")
        term, g_sum, u_sum = sem("term"), sem("g_sum"), sem("u_sum")
        summed, centred, squared, stats = sem("summed"), sem("centred"), sem("squared"), sem("stats")
        normed, relu = sem("normed"), sem("relu")
        hT_ps, hT_hi, hT_lo = sem("hT_ps"), sem("hT_hi"), sem("hT_lo")
        proj, proj_hi, proj_lo = sem("proj"), sem("proj_hi"), sem("proj_lo")
        res_ready = sem("res_ready")
        bb_ps, bb_kept, c_ready = sem("bb_ps"), sem("bb_kept"), sem("c_ready")
        deg_part, deg_sum = sem("deg_part"), sem("deg_sum")
        deg_max = sem("deg_max")
        deg_ps, deg_kept, flag_ready = sem("deg_ps"), sem("deg_kept"), sem("flag_ready")
        counts_final = sem("counts_final")
        gen_ready, gen_used, gen_ps, gen_A, gen_R_s = (sem(n) for n in ("gen_ready", "gen_used", "gen_ps", "gen_A", "gen_R_s"))
        gen_prep, gen_iota, gen_stage, gen_deg = (sem(n) for n in ("gen_prep", "gen_iota", "gen_stage", "gen_deg"))
        agg_stage, agg_used = sem("agg_stage"), sem("agg_used")
        filled, scored, masked, maxed, expd = (sem(n) for n in ("filled", "scored", "masked", "maxed", "expd"))
        pT_ps, pT_hi, pT_lo = sem("pT_ps"), sem("pT_hi"), sem("pT_lo")
        attended, x2_ready, h2_hi, h2_lo, res2_ready = (sem(n) for n in ("attended", "x2_ready", "h2_hi", "h2_lo", "res2_ready"))
        agg_ps, agg_hi, agg_lo = sem("agg_ps"), sem("agg_hi"), sem("agg_lo")
        rdeg_ready, out_ps, out_ready = sem("rdeg_ready"), sem("out_ps"), sem("out_ready")

        def f(ap):
            return ap.bitcast(F32)

        def bcast(ap, dim, n):
            return ap.unsqueeze(dim).broadcast_to([*ap.shape[:dim], n, *ap.shape[dim:]])

        def proj_index(step):
            return PROJ.index(step)

        block = ctx.enter_context(nc.Block())

        @block.sync
        def _(sp):
            for q in range(2):
                for raw, w_d, loaded in ((wq_raw, wqT_d, ld_wq), (wk_raw, wkT_d, ld_wk)):
                    sp.dma_start(raw[:, 2 * q:2 * q + 2, :],
                                 w_d[2 * q * P:(2 * q + 2) * P, :].rearrange("(k p) n -> p k n", p=P)).then_inc(loaded[q], 16)
                if q == 0:
                    sp.dma_start(dst_i[:, :], dst_d).then_inc(ld_edges, 16)
                    sp.dma_start(src_i[:, :], src_d).then_inc(ld_edges, 16)
            for i in range(4):
                sp.dma_start(xs[:, 2 * i:2 * i + 2, :],
                             x_d[2 * i * P:(2 * i + 2) * P, :].rearrange("(t p) n -> p t n", p=P)).then_inc(ld_x[i], 16)
            sp.dma_start(bv_sb[:, :], bv_d.partition_broadcast(P)).then_inc(ld_bv, 16)
            sp.wait_ge(proj, KD)
            sp.dma_start(wv_raw[:, :, :], wv_d.rearrange("(k p) n -> p k n", p=P)).then_inc(ld_wv, 16)
            sp.wait_ge(proj, NPROJ)
            sp.dma_start(b_sb[:, :], b_d.partition_broadcast(P)).then_inc(ld_b, 16)
            sp.wait_ge(counts_final, 1)
            sp.wait_ge(res_ready, NT)
            sp.dma_start(wt_raw[:, :, :], wT_d.rearrange("(k p) n -> p k n", p=P)).then_inc(ld_wt, 16)
            for n, (j, cols) in enumerate(OUT):
                sp.wait_ge(out_ready, n + 1)
                sp.dma_start(out_d[j * P:(j + 1) * P, cols], o_sb[:, j, cols]).then_inc(stored, 16)
            sp.wait_ge(stored, 16 * len(OUT))

        @block.gpsimd
        def _(pool):
            chain = [0]

            def link(ins):
                chain[0] += 1
                ins.then_inc(pool_chain, 1)
                pool.wait_ge(pool_chain, chain[0])

            def weight_lo(n, hl, raw, q, done):
                ks = slice(2 * q, 2 * q + 2)
                pool.wait_ge(w_hi, n)
                nc.gpsimd.tensor_tensor(hl[1][:, ks, :], raw[:, ks, :], f(hl[0][:, ks, :]), ALU.subtract).then_inc(done, 1)

            nc.gpsimd.memset(f(ones_r[:, :]), 1.0).then_inc(consts, 1)
            nc.gpsimd.iota(iota_i[:, 0:NT * WIN], [[1, NT * WIN]], base=0, channel_multiplier=0).then_inc(consts, 1)
            nc.gpsimd.iota(win_i[:, :], [[P, ET // TPB], [WSTEP, TPB]], base=-WBACK, channel_multiplier=0).then_inc(consts, 1)
            link(nc.gpsimd.memset(ident[:, :], 0.0))
            nc.gpsimd.affine_select(out=ident[:, :], in_=ident[:, :], compare_op=ALU.not_equal, fill=1.0, base=0,
                                    pattern=[[-1, P]], channel_multiplier=1).then_inc(consts, 1)
            nc.gpsimd.memset(nhalf[:, :], -0.5).then_inc(consts, 1)
            link(nc.gpsimd.iota(iotaG[:, :, :].bitcast(I32), [[N, NT], [1, GRP]], base=0, channel_multiplier=0))
            nc.gpsimd.tensor_copy(iotaG[:, :, :], iotaG[:, :, :].bitcast(I32)).then_inc(consts, 1)
            weight_lo(4, wk, wk_raw, 1, wk_lo)

            def tile_sum(out, terms, n, done):
                pool.wait_ge(term, KD * n)
                link(nc.gpsimd.tensor_tensor(terms[:, 0:2, :], terms[:, 0:2, :], terms[:, 2:4, :], ALU.add))
                nc.gpsimd.tensor_tensor(out, terms[:, 0, :], terms[:, 1, :], ALU.add).then_inc(done, 1)

            def minus_mean(t):
                pool.wait_ge(summed, t + 1 - STATS0)
                nc.gpsimd.tensor_scalar(nmean[:, t:t + 1], xsum[:, t:t + 1], -1.0 / D, None, ALU.mult).then_inc(centred, 1)

            def inverse_deviation(layer, t):
                link(nc.gpsimd.tensor_tensor(rstd[:, layer, t:t + 1], var_e[:, layer, t:t + 1], nhalf[:, :], ALU.pow))

            def norm0(t):
                pool.wait_ge(squared, t + 1 - STATS0)
                link(nc.gpsimd.tensor_scalar(var_e[:, 0, t:t + 1], xsq[:, t:t + 1], 1.0 / D, EPS, ALU.mult, ALU.add))
                inverse_deviation(0, t)
                nc.gpsimd.tensor_tensor(nmr[:, 0, t:t + 1], nmean[:, t:t + 1], rstd[:, 0, t:t + 1], ALU.mult).then_inc(normed, 1)

            def norm1(layer, t):
                pool.wait_ge(stats, layer * STATS0 + t + 1)
                link(nc.gpsimd.tensor_scalar(var_e[:, layer, t:t + 1], mv[:, t, 1:2], EPS, None, ALU.add))
                inverse_deviation(layer, t)
                nc.gpsimd.tensor_scalar(nmr[:, layer, t:t + 1], mv[:, t, 0:1], rstd[:, layer, t:t + 1], -1.0,
                                        ALU.mult, ALU.mult).then_inc(normed, 1)

            def add_bv(t):
                pool.wait_ge(relu, t + 1)
                nc.gpsimd.tensor_tensor(xs[:, t, :], xs[:, t, :], bv_sb[:, :], ALU.add).then_inc(res_ready, 1)

            pool.wait_ge(consts, 5)
            for step, n, *to in STEPS:
                if step == "stats":
                    norm1(0, n)
                elif step == "sum":
                    minus_mean(n)
                elif step == "squares":
                    norm0(n)
                elif step == "wv":
                    weight_lo(5 + n, wv, wv_raw, n, wv_lo)
                elif step == "c":
                    pool.wait_ge(relu, n + 1)
                    pool.wait_ge(proj_hi, hi_before(proj_index(("u", 0)) + 1))
                    if n >= 2:
                        pool.wait_ge(dots, n - 1)
                    nc.gpsimd.tensor_tensor(uh[n % 2][:, :], h1[:, n, :], u_sb[:, :], ALU.mult).then_inc(uh_ready, 1)
                elif step == "gsum":
                    tile_sum(t_g, g_terms, 1, g_sum)
                elif step == "usum":
                    tile_sum(t_u[:, :], u_terms, 2, u_sum)
                elif step == "V":
                    if n == 0:
                        pool.wait_ge(ld_bv, 16)
                    add_bv(n)
                elif step == "count":
                    for g in kept(n, to[0]):
                        pool.wait_ge(count_kept, g + 1)
                        if g == NG // 2:
                            pool.wait_ge(deg_ps, 1)
                        cols = slice(g * GRP, (g + 1) * GRP)
                        link(nc.gpsimd.tensor_tensor(dfold[:, :, :], A_f[:, 0:4, cols], A_f[:, 4:8, cols], ALU.add))
                        link(nc.gpsimd.tensor_tensor(dfold[:, 0:2, :], dfold[:, 0:2, :], dfold[:, 2:4, :], ALU.add))
                        part = slice(g % (NG // 2) * GRP, (g % (NG // 2) + 1) * GRP)
                        nc.gpsimd.tensor_tensor(dpart[:, part], dfold[:, 0, :], dfold[:, 1, :], ALU.add).then_inc(deg_part, 1)
                        pool.wait_ge(deg_part, g + 1)
            pool.wait_ge(ld_b, 32)
            link(nc.gpsimd.tensor_scalar(b_sb[:, :], b_sb[:, :], alpha[:, :], None, ALU.mult))

            def fill(i):
                if i >= 2:
                    pool.wait_ge(pT_ps, 2 * (i - 1))
                else:
                    link(nc.gpsimd.memset(pr[i][:, :], 0.0))
                nc.gpsimd.tensor_scalar(pr[i % 2][:, :], pr[i % 2][:, :], 0.0, negc[:, i:i + 1],
                                        ALU.mult, ALU.add).then_inc(filled, 1)

            pool.wait_ge(c_ready, 1)
            pool.wait_ge(proj, NPROJ)
            fill(0)
            fill(1)
            for i in range(1, NT + 2):
                if i + 1 < NT:
                    fill(i + 1)
                if i >= 2:
                    norm1(1, i - 2)
                    pool.wait_ge(relu, NT + i - 1)
                    link(nc.gpsimd.tensor_tensor(xs[:, i - 2, :], xs[:, i - 2, :], b_sb[:, :], ALU.add))
                    nc.gpsimd.tensor_tensor(xs[:, i - 2, :], xs[:, i - 2, :], h2f[i % 2][:, :],
                                            ALU.add).then_inc(res2_ready, 1)

        @block.scalar
        def _(act):
            act.dma_start(bqk[:, 0, :], bq_d).then_inc(ld_bqk, 16)
            act.dma_start(bqk[:, 1, :], bk_d).then_inc(ld_bqk, 16)
            act.dma_start(alpha[:, :], alpha_d.partition_broadcast(P)).then_inc(ld_b, 16)
            groups = [0]
            his = [0]

            def norm_relu(layer, t, out):
                act.wait_ge(normed, layer * NT + t + 1)
                nc.scalar.activation(out, xs[:, t, :], ACT.Relu, bias=nmr[:, layer, t:t + 1],
                                     scale=rstd[:, layer, t:t + 1]).then_inc(relu, 1)

            for step, n, *to in STEPS:
                if step == "weights":
                    for q in range(2):
                        ks = slice(2 * q, 2 * q + 2)
                        act.wait_ge(ld_wq[q], 16)
                        nc.scalar.activation(wq[0][:, ks, :], wq_raw[:, ks, :], ACT.Copy, scale=SCALE).then_inc(w_hi, 1)
                        act.wait_ge(ld_wk[q], 16)
                        nc.scalar.activation(wk[0][:, ks, :], wk_raw[:, ks, :], ACT.Copy).then_inc(w_hi, 1)
                        if q == 0:
                            act.wait_ge(consts, 2)
                            nc.scalar.activation(iotaL[:, :, :], bcast(iota_i[:, 0:P], 2, BATCH), ACT.Copy).then_inc(tables, 1)
                            nc.scalar.activation(iotaW[:, :, :], bcast(iota_i[:, 0:NT * WIN], 2, BATCH), ACT.Copy,
                                                 bias=1.0).then_inc(tables, 1)
                elif step == "gterms":
                    act.wait_ge(vec_ready, 1)
                    for k in range(KD):
                        nc.scalar.activation(g_terms[:, k, :], wk_raw[:, k, :], ACT.Copy,
                                             scale=bqk_s[:, 0, k:k + 1]).then_inc(term, 1)
                elif step == "usum":
                    act.wait_ge(proj, KD)
                    for k in range(KD):
                        nc.scalar.activation(u_terms[:, k, :], wq_raw[:, k, :], ACT.Copy,
                                             scale=bqk_s[:, 1, k:k + 1]).then_inc(term, 1)
                elif step == "sum":
                    if n % 2 == 0:
                        act.wait_ge(ld_x[n // 2], 16)
                    nc.scalar.activation(h1[:, n, :], xs[:, n, :], ACT.Copy, accum_out=xsum[:, n:n + 1]).then_inc(summed, 1)
                elif step == "squares":
                    act.wait_ge(centred, n + 1 - STATS0)
                    nc.scalar.activation(h1[:, n, :], xs[:, n, :], ACT.Square, bias=nmean[:, n:n + 1],
                                         accum_out=xsq[:, n:n + 1]).then_inc(squared, 1)
                elif step == "wv":
                    act.wait_ge(ld_wv, 16)
                    ks = slice(2 * n, 2 * n + 2)
                    nc.scalar.activation(wv[0][:, ks, :], wv_raw[:, ks, :], ACT.Copy).then_inc(w_hi, 1)
                elif step == "csum":
                    act.wait_ge(uh_ready, n + 1)
                    nc.scalar.activation(uh[n % 2][:, :], uh[n % 2][:, :], ACT.Copy,
                                         accum_out=c_f[:, n:n + 1]).then_inc(dots, 1)
                elif step == "rows":
                    norm_relu(0, n, h1[:, n, :])
                elif step == "T":
                    act.wait_ge(hT_ps, n + 1)
                    nc.scalar.activation(hT[0][:, :, n * P:(n + 1) * P],
                                         bank[6 + n % 2][:, :].rearrange("p (k c) -> p k c", k=KD),
                                         ACT.Copy).then_inc(hT_hi, 1)
                elif step == "count":
                    for g in kept(n, to[0]):
                        act.wait_ge(oh_used, LAST[g] // BATCH + 1)
                        nc.scalar.activation(A[:, :, g * GRP:(g + 1) * GRP],
                                             bank[g % 2][:, :].rearrange("p (h d) -> p h d", h=NT),
                                             ACT.Copy).then_inc(count_kept, 1)
                elif step == "deg":
                    act.wait_ge(deg_ps, n + 1)
                    nc.scalar.activation(bank[6 + n][0:1, :], bank[6 + n][0:1, :], ACT.Copy,
                                         accum_out=dsum[0:1, n:n + 1]).then_inc(deg_sum, 1)
                elif step in ("M", "u", "G", "V"):
                    i = proj_index((step, n))
                    ps = bank[2 + i % 4]
                    act.wait_ge(proj, i + 1)
                    if step == "M":
                        nc.scalar.activation(M[0][:, n, :], ps[:, :], ACT.Copy).then_inc(proj_hi, 1)
                    elif step == "u":
                        nc.scalar.activation(u_sb[:, :], ps[:, :], ACT.Copy).then_inc(proj_hi, 1)
                    elif step == "G":
                        half, m = n // KD, n % KD
                        if n == 0:
                            act.wait_ge(proj_lo, proj_index(("g", 0)) + 1)
                        nc.scalar.activation(GT[0][:, 4 * half:4 * half + 4, m, :],
                                             ps[:, :].rearrange("p (t c) -> p t c", t=4),
                                             ACT.Identity, bias=g0[:, m:m + 1]).then_inc(proj_hi, 1)
                    else:
                        act.wait_ge(uh_ready, n + 1)
                        nc.scalar.activation(V[0][:, n, :], ps[:, :], ACT.Copy).then_inc(proj_hi, 1)

            for i in range(NT + 2):
                if 1 <= i <= NT:
                    j = i - 1
                    if j >= 2:
                        act.wait_ge(attended, j - 1)
                    for q in range(2):
                        act.wait_ge(pT_ps, 2 * j + q + 1)
                        nc.scalar.activation(pT[j % 2][0][:, 4 * q:4 * q + 4, :],
                                             bank[q][:, :].rearrange("p (b c) -> p b c", b=4),
                                             ACT.Copy).then_inc(pT_hi, 1)
                if i < NT:
                    act.wait_ge(maxed, i + 1)
                    nc.scalar.activation(pr[i % 2][:, :], pr[i % 2][:, :], ACT.Exp, bias=negmax[:, i:i + 1],
                                         accum_out=rowsum[:, i:i + 1]).then_inc(expd, 1)
                if i == 3:
                    act.wait_ge(ld_wt, 16)
                    nc.scalar.activation(wt[0][:, :, :], wt_raw[:, :, :], ACT.Copy).then_inc(w_hi, 1)
                if i >= 2:
                    j = i - 2
                    if j >= 2:
                        act.wait_ge(h2_lo, j - 1)
                        act.wait_ge(res2_ready, j - 1)
                    norm_relu(1, j, h2f[j % 2][:, :])
                    act.wait_ge(relu, NT + j + 1)
                    nc.scalar.activation(h2[0][:, j, :], h2f[j % 2][:, :], ACT.Copy).then_inc(h2_hi, 1)

            for n in range(2 * KD):
                half, m = n // KD, n % KD
                act.wait_ge(agg_ps, n + 1)
                nc.scalar.activation(agT[0][:, m, half * HALF:(half + 1) * HALF], bank[AGG_BANK[n]][:, :],
                                     ACT.Copy).then_inc(agg_hi, 1)

        @block.vector
        def _(dve):
            chain = [0]

            def link(ins):
                chain[0] += 1
                ins.then_inc(dve_chain, 1)
                dve.wait_ge(dve_chain, chain[0])

            def edge_keys():
                dve.wait_ge(ld_edges, 32)
                nc.vector.tensor_scalar(key_i[0][:, :], src_i[:, :], P - 1, None, ALU.bitwise_and)
                nc.vector.tensor_scalar(key_i[1][:, :], src_i[:, :], N - P, None, ALU.bitwise_and)
                dve.wait_ge(consts, 3)
                link(nc.vector.tensor_scalar(win0[:, :], win_i[:, :], 0.0, float(N - WIN), ALU.max, ALU.min))
                link(nc.vector.tensor_tensor(key_t[0][:, :], dst_i[:, :], win0[:, :], ALU.subtract))
                nc.vector.tensor_copy(lo_b[:, :], key_i[0][:, :])
                nc.vector.scalar_tensor_tensor(out=key_t[1][:, :], in0=key_i[1][:, :], scalar=float(WIN) / P,
                                               in1=key_t[0][:, :], op0=ALU.mult, op1=ALU.add)
                link(nc.vector.tensor_scalar(key_t[2][:, :], key_t[0][:, :], float(WIN), None, ALU.is_lt))
                link(nc.vector.scalar_tensor_tensor(out=key_t[3][:, :], in0=key_t[0][:, :], scalar=0.0,
                                                    in1=key_t[2][:, :], op0=ALU.is_ge, op1=ALU.mult))
                link(nc.vector.scalar_tensor_tensor(out=key_b[:, :], in0=key_t[1][:, :], scalar=1.0,
                                                    in1=key_t[3][:, :], op0=ALU.add, op1=ALU.mult))
                dve.wait_ge(tables, 2)

            def one_hots(a, b):
                for q in range(a, b):
                    if q >= RING:
                        dve.wait_ge(oh_used, q - RING + 1)
                    tiles = slice(BATCH * q, BATCH * q + BATCH)
                    nc.vector.tensor_tensor(ohL[:, q % RING, :, :], iotaL[:, :, :], bcast(lo_b[:, tiles], 1, P), ALU.is_equal)
                    nc.vector.tensor_tensor(ohW[:, q % RING, :, :, :].rearrange("p h d b -> p (h d) b"), iotaW[:, :, :],
                                            bcast(key_b[:, tiles], 1, NT * WIN), ALU.is_equal).then_inc(oh_ready, 1)

            def row_stats(t):
                link(nc.vector.bn_stats(bn[:, t, :], xs[:, t, :]))
                nc.vector.bn_aggr(mv[:, t, :], bn[:, t, :]).then_inc(stats, 1)

            def stats0(t):
                if t % 2 == 0:
                    dve.wait_ge(ld_x[t // 2], 16)
                row_stats(t)

            def split_lo(n, hl, raw, ks=slice(0, KD), scale=1.0):
                dve.wait_ge(w_hi, n)
                nc.vector.scalar_tensor_tensor(out=hl[1][:, ks, :], in0=raw[:, ks, :], scalar=scale, in1=f(hl[0][:, ks, :]),
                                               op0=ALU.mult, op1=ALU.subtract).then_inc(w_lo, 1)

            for step, n, *to in VSTEPS:
                if step == "weights":
                    split_lo(1, wq, wq_raw, slice(0, 2), SCALE)
                    split_lo(2, wk, wk_raw, slice(0, 2))
                    edge_keys()
                    dve.wait_ge(ld_bqk, 32)
                    link(nc.vector.tensor_scalar(bqk_s[:, :, :], bqk[:, :, :], SCALE, None, ALU.mult))
                    nc.vector.tensor_tensor(bprod[:, :], bqk_s[:, 0, :], bqk[:, 1, :], ALU.mult).then_inc(vec_ready, 1)
                    one_hots(0, START)
                    split_lo(3, wq, wq_raw, slice(2, 4), SCALE)
                elif step == "count":
                    one_hots(max(n, START), to[0])
                elif step in ("sum", "squares", "rows", "Ma", "gterms", "gsum", "usum", "wv", "c"):
                    pass
                elif step == "stats":
                    stats0(n)
                elif step == "deg":
                    dve.wait_ge(deg_sum, n + 1)
                    nc.vector.tensor_reduce(dmax[0:1, n:n + 1], bank[6 + n][0:1, :], AX.X, ALU.max).then_inc(deg_max, 1)
                elif step == "T":
                    dve.wait_ge(hT_hi, n + 1)
                    hi = hT[0][:, :, n * P:(n + 1) * P]
                    nc.vector.tensor_tensor(hT[1][:, :, n * P:(n + 1) * P],
                                            bank[6 + n % 2][:, :].rearrange("p (k c) -> p k c", k=KD), f(hi),
                                            ALU.subtract).then_inc(hT_lo, 1)
                elif step == "g":
                    i = proj_index((step, n))
                    dve.wait_ge(proj, i + 1)
                    nc.vector.tensor_copy(g0[:, :], bank[2 + i % 4][:, 0:KD]).then_inc(proj_lo, 1)
                elif step == "u":
                    i = proj_index((step, n))
                    dve.wait_ge(proj_hi, hi_before(i + 1))
                    nc.vector.memset(dbad[:, :], 0.0).then_inc(proj_lo, 1)
                elif step == "csum":
                    if n == NT - 1:
                        dve.wait_ge(dots, NT)
                        dve.wait_ge(bb_kept, 1)
                        link(nc.vector.tensor_scalar(negc[:, :], c_f[:, :], bb[:, :], None, ALU.add))
                        nc.vector.tensor_scalar(negc[:, :], negc[:, :], -1.0, NEG, ALU.mult, ALU.add).then_inc(c_ready, 1)
                else:
                    i = proj_index((step, n))
                    ps = bank[2 + i % 4]
                    dve.wait_ge(proj_hi, hi_before(i + 1))
                    if (step, n) == ("M", 0):
                        dve.wait_ge(bb_ps, 1)
                        nc.vector.tensor_reduce(bb[:, :], bank[7][:, 0:KD], AX.X, ALU.add).then_inc(bb_kept, 1)
                    if step == "M":
                        ins = nc.vector.tensor_tensor(M[1][:, n, :], ps[:, :], f(M[0][:, n, :]), ALU.subtract)
                    elif step == "G":
                        half, m = n // KD, n % KD
                        ins = nc.vector.scalar_tensor_tensor(
                            out=GT[1][:, 4 * half:4 * half + 4, m, :], in0=ps[:, :].rearrange("p (t c) -> p t c", t=4),
                            scalar=g0[:, m:m + 1], in1=f(GT[0][:, 4 * half:4 * half + 4, m, :]),
                            op0=ALU.add, op1=ALU.subtract)
                    else:
                        ins = nc.vector.tensor_tensor(V[1][:, n, :], ps[:, :], f(V[0][:, n, :]), ALU.subtract)
                    ins.then_inc(proj_lo, 1)

            dve.wait_ge(deg_max, 2)
            nc.vector.tensor_scalar(dbad[0:1, 0:1], dsum[0:1, 0:1], dsum[0:1, 1:2], float(E), ALU.add, ALU.not_equal)
            link(nc.vector.tensor_scalar(dbad[0:1, 1:2], dmax[0:1, 0:1], dmax[0:1, 1:2], float(EXACT), ALU.max, ALU.is_ge))
            nc.vector.tensor_tensor(flag[0:1, :], dbad[0:1, 0:1], dbad[0:1, 1:2], ALU.add).then_inc(flag_ready, 1)
            dve.wait_ge(flag_ready, 1)
            general = nc.vector.value_load(flag[0:1, 0:1], min_val=0, max_val=2)
            with dve.If(general > 0):
                dve.wait_ge(res_ready, NT)
                nc.vector.tensor_scalar(gen_key[:, :].bitcast(I32), src_i[:, :], P - 1, None, ALU.bitwise_and).then_inc(gen_prep, 1)
                dve.wait_ge(gen_prep, 1)
                nc.vector.tensor_copy(gen_lo[:, :], gen_key[:, :].bitcast(I32)).then_inc(gen_prep, 1)
                dve.wait_ge(gen_prep, 2)
                nc.vector.memset(gen0[:, :], 0.0)
                nc.vector.tensor_scalar(gen_i[:, :], src_i[:, :], N - P, None, ALU.bitwise_and).then_inc(gen_prep, 1)
                dve.wait_ge(gen_prep, 3)
                nc.vector.scalar_tensor_tensor(out=gen_key[:, :], in0=gen_i[:, :], scalar=float(N) / P, in1=dst_i[:, :],
                                               op0=ALU.mult, op1=ALU.add).then_inc(gen_prep, 1)
                nc.vector.memset(dbad[:, :], 0.0).then_inc(gen_R_s, 1)
                dve.wait_ge(gen_prep, 4)
                dve.wait_ge(consts, 6)
                with dve.Fori(0, NG) as g:
                    with dve.Fori(0, (ET // 2)) as q:
                        dve.wait_ge(gen_used, g * (ET // 2) + q + 1)
                        for u in range(2):
                            nc.vector.tensor_scalar(genL[:, u, :], iotaL[:, :, 0], gen_lo[:, bass.ds(2 * q + u, 1)], None,
                                                    ALU.is_equal)
                            last = nc.vector.tensor_scalar(genW[:, u, :], iotaG[:, :, :].rearrange("p h d -> p (h d)"),
                                                           gen_key[:, bass.ds(2 * q + u, 1)], None, ALU.is_equal)
                        last.then_inc(gen_ready, 1)
                    nc.vector.tensor_scalar(iotaG[:, :, :], iotaG[:, :, :], float(GRP), None, ALU.add).then_inc(gen_iota, 1)
                    dve.wait_ge(gen_ps, g + 1)
                    got = bank[0][:, :].rearrange("p (h d) -> p h d", h=NT)
                    nc.vector.tensor_copy(A[:, :, bass.ds(g * GRP, GRP)], got).then_inc(gen_A, 1)
                    dve.wait_ge(gen_A, g + 1)
                    nc.vector.tensor_tensor(R[:, :, bass.ds(g * GRP, GRP)], got, A_f[:, :, bass.ds(g * GRP, GRP)],
                                            ALU.subtract).then_inc(gen_R_s, 1)
                    dve.wait_ge(gen_iota, g + 1)
                    dve.wait_ge(gen_R_s, g + 2)
                for h in range(NT):
                    if h:
                        dve.wait_ge(gen_deg, h)
                    nc.vector.tensor_copy(gen_R[:, :], R[:, h, :]).then_inc(gen_stage, 1)
                dve.wait_ge(gen_deg, NT)
            nc.vector.memset(dbad[:, :], 0.0).then_inc(counts_final, 1)

            def degree_columns():
                for j in range(NT):
                    ins = nc.vector.tensor_tensor_reduce(
                        out=diag_d[:, :], in0=bank[6 + j // 4][:, j % 4 * P:(j % 4 + 1) * P], in1=ident[:, :], scale=1.0,
                        scalar=0.0, op0=ALU.mult, op1=ALU.add, accum_out=deg[:, j:j + 1])
                    if j < NT - 1:
                        link(ins)
                ins.then_inc(deg_kept, 1)
                dve.wait_ge(deg_kept, 1)
                link(nc.vector.tensor_scalar(deg[:, :], deg[:, :], 1.0, None, ALU.max))
                nc.vector.reciprocal(rdeg[:, :], deg[:, :]).then_inc(rdeg_ready, 1)

            degree_columns()

            def h2_lo_part(j):
                dve.wait_ge(h2_hi, j + 1)
                nc.vector.tensor_tensor(h2[1][:, j, :], h2f[j % 2][:, :], f(h2[0][:, j, :]), ALU.subtract).then_inc(h2_lo, 1)

            for i in range(NT + 2):
                if i < NT:
                    dve.wait_ge(filled, i + 1)
                    for q in range(2):
                        dve.wait_ge(scored, 2 * i + q + 1)
                        cols = slice(q * HALF, (q + 1) * HALF)
                        ins = nc.vector.copy_predicated(pr[i % 2][:, cols], A_i[:, i, cols], bank[2 + (2 * i + q) % 4][:, :])
                        ins.then_inc(masked, 1)
                    dve.wait_ge(masked, 2 * i + 2)
                    nc.vector.tensor_reduce(negmax[:, i:i + 1], pr[i % 2][:, :], AX.X, ALU.max, negate=True).then_inc(maxed, 1)
                if i == 3:
                    dve.wait_ge(ld_b, 32)
                    dve.wait_ge(rdeg_ready, 1)
                    nc.vector.tensor_scalar(rdeg[:, :], rdeg[:, :], alpha[:, :], None, ALU.mult).then_inc(rdeg_ready, 1)
                    dve.wait_ge(ld_wt, 16)
                    split_lo(7, wt, wt_raw)
                if 1 <= i <= NT:
                    j = i - 1
                    for q in range(2):
                        dve.wait_ge(pT_hi, 2 * j + q + 1)
                        nc.vector.tensor_tensor(pT[j % 2][1][:, 4 * q:4 * q + 4, :],
                                                bank[q][:, :].rearrange("p (b c) -> p b c", b=4),
                                                f(pT[j % 2][0][:, 4 * q:4 * q + 4, :]), ALU.subtract).then_inc(pT_lo, 1)
                if i >= 3:
                    h2_lo_part(i - 3)
                if i >= 2:
                    j = i - 2
                    dve.wait_ge(expd, j + 1)
                    link(nc.vector.reciprocal(rinv[:, j:j + 1], rowsum[:, j:j + 1]))
                    dve.wait_ge(attended, j + 1)
                    nc.vector.scalar_tensor_tensor(out=xs[:, j, :], in0=bank[6 + j % 2][:, :], scalar=rinv[:, j:j + 1],
                                                   in1=xs[:, j, :], op0=ALU.mult, op1=ALU.add).then_inc(x2_ready, 1)
                    dve.wait_ge(x2_ready, j + 1)
                    row_stats(j)
            h2_lo_part(NT - 1)

            with dve.If(general > 0):
                for k in range(2 * NT):
                    half, h = k // NT, k % NT
                    if k == 0:
                        dve.wait_ge(h2_lo, NT)
                        dve.wait_ge(res2_ready, NT)
                    if k >= 2:
                        dve.wait_ge(agg_used, k - 1)
                    nc.vector.tensor_copy(r_st[k % 2][:, :], R[:, h, half * HALF:(half + 1) * HALF]).then_inc(agg_stage, 1)

            for n in range(2 * KD):
                half, m = n // KD, n % KD
                cols = slice(half * HALF, (half + 1) * HALF)
                dve.wait_ge(agg_hi, n + 1)
                nc.vector.tensor_tensor(agT[1][:, m, cols], bank[AGG_BANK[n]][:, :], f(agT[0][:, m, cols]),
                                        ALU.subtract).then_inc(agg_lo, 1)
            dve.wait_ge(rdeg_ready, 2)
            for n, (j, cols) in enumerate(OUT):
                dve.wait_ge(res2_ready, j + 1)
                dve.wait_ge(out_ps, n + 1)
                nc.vector.scalar_tensor_tensor(out=o_sb[:, j, cols], in0=bank[OUT_BANK[n]][:, cols], scalar=rdeg[:, j:j + 1],
                                               in1=xs[:, j, cols], op0=ALU.mult, op1=ALU.add).then_inc(out_ready, 1)

        @block.tensor
        def _(pe):
            mm = nc.tensor.matmul

            pe.wait_ge(consts, 1)
            for _ in range(WARM):
                mm(bank[7][:, 0:P], ones_r[:, :], ones_r[:, :], start=True, stop=True)

            def product(out, lhs, rhs, pairs, first, final):
                for k, (a, b) in enumerate(pairs):
                    mm(out, lhs[0][a], rhs[0][b], start=(first and k == 0), stop=False)
                    mm(out, lhs[0][a], rhs[1][b], start=False, stop=False)
                    last = mm(out, lhs[1][a], rhs[0][b], start=False, stop=(final and k == len(pairs) - 1))
                return last

            def three_pass(out, lhs, rhs, pairs):
                return product(out, lhs, rhs, pairs, True, True)

            def count(a, b):
                for q in range(a, b):
                    pe.wait_ge(oh_ready, q + 1)
                    for u in range(BATCH):
                        t = BATCH * q + u
                        w = window(t)
                        for g, c0, c1 in pieces(t):
                            if FIRST[g] == t and g >= 2:
                                pe.wait_ge(count_kept, g - 1)
                            out = bank[g % 2][:, :].rearrange("p (h d) -> p h d", h=NT)[:, :, c0 - g * GRP:c1 - g * GRP]
                            last = mm(out, ohL[:, q % RING, :, u], ohW[:, q % RING, :, c0 - w:c1 - w, u],
                                      start=(FIRST[g] == t), stop=(LAST[g] == t), skip_group_check=True)
                    last.then_inc(oh_used, 1)

            def degrees(rows, q, first, stop):
                for n, row in enumerate(rows):
                    last = mm(bank[6 + q][:, :], ones_r[:, :], row, start=(first and n == 0),
                              stop=stop and n == len(rows) - 1, skip_group_check=True)
                return last

            every = slice(None)

            def cols(k, m, width=P):
                return (every, k, slice(m * width, (m + 1) * width))

            for step, n, *to in STEPS:
                if step == "count":
                    count(n, to[0])
                elif step == "T":
                    pe.wait_ge(relu, n + 1)
                    if n == 0:
                        pe.wait_ge(consts, 4)
                    if n == 1:
                        pe.wait_ge(bb_kept, 1)
                    if n >= 2:
                        pe.wait_ge(hT_lo, n - 1)
                    for k in range(KD):
                        last = nc.tensor.transpose(bank[6 + n % 2][:, k * P:(k + 1) * P], h1[:, n, k * P:(k + 1) * P],
                                                   ident[:, :])
                    last.then_inc(hT_ps, 1)
                elif step == "deg":
                    pe.wait_ge(deg_part, NG // 2 * (n + 1))
                    pe.wait_ge(hT_lo, NT)
                    degrees([dpart[:, :]], n, True, True).then_inc(deg_ps, 1)
                elif step == "Ma":
                    pe.wait_ge(w_lo, 2)
                    for m in (2 * n, 2 * n + 1):
                        product(bank[2 + m][:, :], wq, wk, [(cols(k, m), cols(k, 0, D)) for k in (0, 1)], True, False)
                elif step in ("M", "u", "g", "G", "V"):
                    i = proj_index((step, n))
                    ps = bank[2 + i % 4]
                    if i >= 4:
                        pe.wait_ge(proj_lo, i - 3)
                    if step == "M":
                        pe.wait_ge(w_lo, 3)
                        pe.wait_ge(wk_lo, 1)
                        if n == 0:
                            pe.wait_ge(vec_ready, 1)
                            mm(bank[7][:, 0:KD], f(ones_r[:, :]), bprod[:, :], start=True, stop=True).then_inc(bb_ps, 1)
                        last = product(ps[:, :], wq, wk, [(cols(k, n), cols(k, 0, D)) for k in (2, 3)], False, True)
                    elif step == "u":
                        pe.wait_ge(u_sum, 1)
                        last = mm(ps[:, :], f(ones_r[:, :]), t_u[:, :], start=True, stop=True)
                    elif step == "g":
                        pe.wait_ge(g_sum, 1)
                        for m in range(KD):
                            last = mm(ps[:, m:m + 1], t_g[:, m * P:(m + 1) * P], f(ones_r[:, 0:1]), start=True, stop=True)
                    elif step == "G":
                        half, m = n // KD, n % KD
                        if m == 0:
                            pe.wait_ge(hT_lo, 4 * (half + 1))
                            pe.wait_ge(proj_lo, KD)
                        last = three_pass(ps[:, :], M, hT, [(cols(k, m), cols(k, half, HALF)) for k in range(KD)])
                    else:
                        if n == 0:
                            pe.wait_ge(wv_lo, 2)
                        last = three_pass(ps[:, :], hT, wv, [(cols(k, n), cols(k, 0, D)) for k in range(KD)])
                    last.then_inc(proj, 1)

            def scores(i):
                for q in range(2):
                    if i < 2:
                        pe.wait_ge(proj_lo, max(n + 1 for n in range(NPROJ) if n % 4 == 2 * i + q))
                    else:
                        pe.wait_ge(masked, 2 * (i - 2) + q + 1)
                    three_pass(bank[2 + (2 * i + q) % 4][:, :], GT, hT,
                               [((every, i, k, every), cols(k, q, HALF)) for k in range(KD)]).then_inc(scored, 1)

            scores(0)
            scores(1)
            pe.wait_ge(flag_ready, 1)
            general = nc.tensor.value_load(flag[0:1, 0:1], min_val=0, max_val=2)
            with pe.If(general > 0):
                pe.wait_ge(gen_prep, 4)
                mm(bank[0][:, 0:P], gen0[:, 0:P], gen0[:, 0:P], start=True, stop=True).then_inc(gen_used, 1)
                with pe.Fori(0, NG) as g:
                    pe.wait_ge(gen_R_s, g + 1)
                    mm(bank[0][:, :], gen0[:, 0:P], gen0[:, :], start=True, stop=False, skip_group_check=True)
                    with pe.Fori(0, (ET // 2)) as q:
                        pe.wait_ge(gen_ready, g * (ET // 2) + q + 1)
                        for u in range(2):
                            last = mm(bank[0][:, :], genL[:, u, :], genW[:, u, :], start=False, stop=False,
                                      skip_group_check=True)
                        last.then_inc(gen_used, 1)
                    mm(bank[0][:, :], gen0[:, 0:P], gen0[:, :], start=False, stop=True,
                       skip_group_check=True).then_inc(gen_ps, 1)
                pe.wait_ge(gen_R_s, NG + 1)
                for q in range(2):
                    degrees([A[:, h, q * HALF:(q + 1) * HALF] for h in range(NT)], q, True, False)
                for h in range(NT):
                    pe.wait_ge(gen_stage, h + 1)
                    for q in range(2):
                        last = degrees([gen_R[:, q * HALF:(q + 1) * HALF]], q, False, h == NT - 1)
                    last.then_inc(gen_deg, 1)

            def aggregate(rows, groups):
                for h in rows:
                    if groups[0] == 0:
                        pe.wait_ge(h2_lo, h + 1)
                        if h == 0:
                            pe.wait_ge(masked, 2 * NT)
                    for n in groups:
                        half, m = n // KD, n % KD
                        for hl in range(2):
                            last = mm(bank[AGG_BANK[n]][:, :], h2[hl][:, h, m * P:(m + 1) * P],
                                      A[:, h, half * HALF:(half + 1) * HALF], start=(h == 0 and hl == 0),
                                      stop=(h == NT - 1 and hl == 1), skip_group_check=True)
                        if h == NT - 1:
                            last.then_inc(agg_ps, 1)

            for i in range(NT + 2):
                if 2 <= i < NT:
                    scores(i)
                if 1 <= i <= NT:
                    j = i - 1
                    pe.wait_ge(expd, j + 1)
                    if j == 0:
                        pe.wait_ge(counts_final, 1)
                    for q in range(2):
                        if j >= 1:
                            pe.wait_ge(pT_lo, 2 * (j - 1) + q + 1)
                        for b in range(4):
                            c = (4 * q + b) * P
                            last = nc.tensor.transpose(bank[q][:, b * P:(b + 1) * P], pr[j % 2][:, c:c + P], ident[:, :])
                        last.then_inc(pT_ps, 1)
                if i >= 2:
                    j = i - 2
                    if j < NT - 1:
                        pe.wait_ge(pT_lo, 2 * (j + 1))
                    if j == 0:
                        pe.wait_ge(deg_kept, 1)
                    if j >= 2:
                        pe.wait_ge(x2_ready, j - 1)
                    if i == NT + 1:
                        aggregate(range(0, NT - 2), range(0, KD))
                        pe.wait_ge(pT_lo, 2 * NT)
                    three_pass(bank[6 + j % 2][:, :], pT[j % 2], V,
                               [((every, b, every), (every, b, every)) for b in range(NT)]).then_inc(attended, 1)

            aggregate(range(NT - 2, NT - 1), range(0, KD))
            pe.wait_ge(x2_ready, NT)
            aggregate(range(0, NT - 2), range(KD, 2 * KD))
            pe.wait_ge(h2_lo, NT)
            with pe.If(general > 0):
                for k in range(2 * NT):
                    half, h = k // NT, k % NT
                    pe.wait_ge(agg_stage, k + 1)
                    for m in range(KD):
                        for hl in range(2):
                            last = mm(bank[AGG_BANK[half * KD + m]][:, :], h2[hl][:, h, m * P:(m + 1) * P],
                                      r_st[k % 2][:, :], start=False, stop=False, skip_group_check=True)
                    last.then_inc(agg_used, 1)
            aggregate(range(NT - 1, NT), range(0, KD))
            aggregate(range(NT - 2, NT), range(KD, 2 * KD))

            pe.wait_ge(w_lo, 4)
            for n, (j, part) in enumerate(OUT):
                if n % 4 == 0 and j < NT:
                    pe.wait_ge(agg_lo, KD * min(n // 4 + 1, 2))
                if n >= 4 and OUT_BANK[n] == OUT_BANK[n - 4]:
                    pe.wait_ge(out_ready, n - 3)
                three_pass(bank[OUT_BANK[n]][:, part], agT, wt,
                           [(cols(k, j), (every, k, part)) for k in range(KD)]).then_inc(out_ps, 1)


OUT = [(j, slice(0, D)) for j in range(NT - 1)] + [(NT - 1, slice(0, D // 2)), (NT - 1, slice(D // 2, D))]
OUT_BANK = [2 + n % 4 for n in range(NT)] + [0]
AGG_BANK = [2, 3, 4, 5, 0, 1, 6, 7]


def kernel(**inputs):
    import numpy as _np
    import concourse.bacc as _bacc
    from concourse import mybir as _mybir
    from concourse.bass_utils import run_bass_kernel_spmd as _run

    def columns(v):
        return _np.asarray(v).reshape(-1, P).T

    layout = {
        "x": _np.asarray(inputs["x"]),
        "src": columns(inputs["src"]), "dst": columns(inputs["dst"]),
        "wqT": _np.asarray(inputs["L0_gnn_Wq"]).T, "wkT": _np.asarray(inputs["L0_gnn_Wk"]).T,
        "wv": _np.asarray(inputs["L0_gnn_Wv"]), "wT": _np.asarray(inputs["L1_gnn_W"]).T,
        "bq": columns(inputs["L0_gnn_bq"]), "bk": columns(inputs["L0_gnn_bk"]),
        "bv": _np.asarray(inputs["L0_gnn_bv"]), "b": _np.asarray(inputs["L1_gnn_b"]),
        "alpha": _np.asarray(inputs["L1_gnn_alpha"]).reshape(1),
    }
    nc = _bacc.Bacc("TRN2", target_bir_lowering=False, num_devices=1)
    arrays, args = {}, []
    for name, a in layout.items():
        a = _np.ascontiguousarray(a)
        arrays[f"in_{name}"] = a
        args.append(nc.dram_tensor(f"in_{name}", a.shape, _mybir.dt.from_np(a.dtype), kind="ExternalInput").ap())
    out = nc.dram_tensor("out_dram", (N, D), _mybir.dt.float32, kind="ExternalOutput").ap()
    gnn_kernel(nc, *args, out)
    r = _run(nc, [arrays], core_ids=[0])
    return r.results[0]["out_dram"]
```
